# Optimizing a Trainium2 kernel written in Bass

```python
import numpy as np
import jax
import jax.numpy as jnp

def _softmax(x, axis=-1):
    return jax.nn.softmax(x, axis=axis)

def _gelu(x):
    return jax.nn.gelu(x, approximate=True)

def _silu(x):
    return jax.nn.silu(x)

def _sigmoid(x):
    return jax.nn.sigmoid(x)

def _layernorm(x, axis=-1, eps=1e-05):
    m = jnp.mean(x, axis=axis, keepdims=True)
    v = jnp.var(x, axis=axis, keepdims=True)
    return (x - m) / jnp.sqrt(v + eps)

def _scatter_add(tgt, idx, src, axis=0):
    return tgt.at[idx].add(src)

def _segment_sum(src, seg, n):
    return jax.ops.segment_sum(src, seg, n)
kernel_name = 'mk_xattn_seq_d2_seqx_r4_f3688b'

def setup_inputs(seed: int=0):
    np.random.seed(seed)
    _w = jnp.asarray

    def _rec_inputs():
        import jax
        import jax.numpy as jnp
        _rk = jax.random.key(seed)
        x = 7.22e-05 + 1 * jax.random.normal(jax.random.fold_in(_rk, 1), (16, 128, 512), jnp.float32)
        _lenS = 128 - jax.random.randint(jax.random.fold_in(_rk, 7), (16,), 0, max(1, 128 // 4) + 1, jnp.int32)
        _lenS2 = 128 - jax.random.randint(jax.random.fold_in(_rk, 8), (16,), 0, max(1, 128 // 4) + 1, jnp.int32)
        _ctx_2048P = jax.random.normal(jax.random.fold_in(_rk, 11), (16, 16, 512), jnp.float32)
        _ctx_2048c = jax.random.dirichlet(jax.random.fold_in(_rk, 511), 0.3 * jnp.ones((16,), jnp.float32), (16, 128))
        _ctx_2048t = jnp.einsum('bsk,bkd->bsd', _ctx_2048c, _ctx_2048P)
        _ctx_2048t = _ctx_2048t * jax.lax.rsqrt(jnp.mean(jnp.square(_ctx_2048t)) + 1e-12) * 0.953939
        ctx_2048 = 4.13588e-05 + 0.999923 * (_ctx_2048t + 0.3 * jax.random.normal(jax.random.fold_in(_rk, 611), (16, 128, 512), jnp.float32))
        _validS = jnp.arange(128)[None, :] < _lenS[:, None]
        _validS2 = jnp.arange(128)[None, :] < _lenS2[:, None]
        _causal = jnp.tril(jnp.ones((128, 128), dtype=bool))
        mask_Bx1xSxS2_ff0 = jnp.where(jnp.ones((16, 1, 128, 128), dtype=bool), 0.0, -1000000000.0).astype(jnp.float32)
        return (x, ctx_2048, mask_Bx1xSxS2_ff0)
    x, ctx_2048, mask_Bx1xSxS2_ff0 = _rec_inputs()

    def _L0_xattn_setup():
        import jax, jax.numpy as jnp
        import numpy as np
        H = 512
        NH = 32
        KVH = 8
        HD = H // NH
        GROUPS = NH // KVH
        EPS = 1e-06
        B, L, S = (4, 256, 256)

        def _gqa_forward(hidden_state, encoder_hidden_state, encoder_attention_mask, Wq, bq, Wk, bk, Wv, bv, Wo, bo, gamma, beta):
            b, l, _ = hidden_state.shape
            s = encoder_hidden_state.shape[1]
            q = hidden_state @ Wq + bq
            k = encoder_hidden_state @ Wk + bk
            v = encoder_hidden_state @ Wv + bv
            q = q.reshape(b, l, KVH, GROUPS, HD).transpose(0, 2, 3, 1, 4)
            k = k.reshape(b, s, KVH, HD).transpose(0, 2, 1, 3)
            v = v.reshape(b, s, KVH, HD).transpose(0, 2, 1, 3)
            scale = 1.0 / jnp.sqrt(jnp.asarray(HD, q.dtype))
            scores = jnp.einsum('bkgld,bksd->bkgls', q, k) * scale
            scores = scores + encoder_attention_mask[:, :, None, :, :]
            attn = jax.nn.softmax(scores, axis=-1)
            out = jnp.einsum('bkgls,bksd->bkgld', attn, v)
            out = out.transpose(0, 3, 1, 2, 4).reshape(b, l, H)
            out = out @ Wo + bo
            x = out + hidden_state
            mu = jnp.mean(x, axis=-1, keepdims=True)
            var = jnp.var(x, axis=-1, keepdims=True)
            return (x - mu) * jax.lax.rsqrt(var + EPS) * gamma + beta
        key = jax.random.key(seed)
        ks = jax.random.split(key, 12)
        sd = 0.02
        return {'hidden_state': jax.random.normal(ks[0], (B, L, H), jnp.float32), 'encoder_hidden_state': jax.random.normal(ks[1], (B, S, H), jnp.float32), 'encoder_attention_mask': jnp.zeros((B, 1, L, S), jnp.float32), 'Wq': jax.random.normal(ks[2], (H, H), jnp.float32) * sd, 'bq': jnp.zeros((H,), jnp.float32), 'Wk': jax.random.normal(ks[3], (H, KVH * HD), jnp.float32) * sd, 'bk': jnp.zeros((KVH * HD,), jnp.float32), 'Wv': jax.random.normal(ks[4], (H, KVH * HD), jnp.float32) * sd, 'bv': jnp.zeros((KVH * HD,), jnp.float32), 'Wo': jax.random.normal(ks[5], (H, H), jnp.float32) * sd, 'bo': jnp.zeros((H,), jnp.float32), 'gamma': jnp.ones((H,), jnp.float32), 'beta': jnp.zeros((H,), jnp.float32)}
    _L0_xattn_all = _L0_xattn_setup()
    _L0_xattn_in = {k: v for k, v in _L0_xattn_all.items() if k in ('Wq', 'bq', 'Wk', 'bk', 'Wv', 'bv', 'Wo', 'bo', 'gamma', 'beta')}
    del _L0_xattn_all

    def _L1_xattn_setup():
        import jax, jax.numpy as jnp
        import numpy as np
        B, Q, S1, S2 = (4, 64, 512, 512)
        D, H, K, F = (512, 16, 128, 2048)
        LN_EPS = 1e-05

        def _layer_norm(x, scale, offset):
            mu = jnp.mean(x, axis=-1, keepdims=True)
            var = jnp.var(x, axis=-1, keepdims=True)
            return (x - mu) * jax.lax.rsqrt(var + LN_EPS) * scale + offset

        def _cross_attention(q_in, kv_in, wq, bq, wk, bk, wv, bv, wo, bo, bias_k, bias_v):
            b, q_len, _ = q_in.shape
            t = kv_in.shape[1]
            qh = (q_in @ wq + bq).reshape(b, q_len, H, K)
            kh = (kv_in @ wk + bk).reshape(b, t, H, K)
            vh = (kv_in @ wv + bv).reshape(b, t, H, K)
            kh = jnp.concatenate([kh, jnp.broadcast_to(bias_k, (b, 1, H, K))], axis=1)
            vh = jnp.concatenate([vh, jnp.broadcast_to(bias_v, (b, 1, H, K))], axis=1)
            scale = jnp.sqrt(jnp.asarray(K, q_in.dtype))
            logits = jnp.einsum('bqhk,bthk->bhqt', qh, kh) / scale
            weights = jax.nn.softmax(logits, axis=-1)
            ctx = jnp.einsum('bhqt,bthk->bqhk', weights, vh).reshape(b, q_len, H * K)
            return ctx @ wo + bo

        def _forward(x, xf_1, xf_2, ln1_scale, ln1_offset, wq1, bq1, wk1, bk1, wv1, bv1, wo1, bo1, bias_k1, bias_v1, ln2_scale, ln2_offset, wq2, bq2, wk2, bk2, wv2, bv2, wo2, bo2, bias_k2, bias_v2, ln_mlp_scale, ln_mlp_offset, w_fc1, b_fc1, w_fc2, b_fc2):
            res = x
            h = _layer_norm(x, ln1_scale, ln1_offset)
            x = res + _cross_attention(h, xf_1, wq1, bq1, wk1, bk1, wv1, bv1, wo1, bo1, bias_k1, bias_v1)
            res = x
            h = _layer_norm(x, ln2_scale, ln2_offset)
            x = res + _cross_attention(h, xf_2, wq2, bq2, wk2, bk2, wv2, bv2, wo2, bo2, bias_k2, bias_v2)
            h = _layer_norm(x, ln_mlp_scale, ln_mlp_offset)
            h = jax.nn.gelu(h @ w_fc1 + b_fc1, approximate=False) @ w_fc2 + b_fc2
            return x + h
        key = jax.random.key(seed)
        ks = iter(jax.random.split(key, 64))

        def rn(shape, s=0.02):
            return jax.random.normal(next(ks), shape, jnp.float32) * s
        inp = {'x': rn((B, Q, D), 1.0), 'xf_1': rn((B, S1, D), 1.0), 'xf_2': rn((B, S2, D), 1.0)}
        for i in (1, 2):
            inp[f'ln{i}_scale'] = jnp.ones((D,), jnp.float32)
            inp[f'ln{i}_offset'] = jnp.zeros((D,), jnp.float32)
            inp[f'wq{i}'] = rn((D, H * K))
            inp[f'bq{i}'] = jnp.zeros((H * K,), jnp.float32)
            inp[f'wk{i}'] = rn((D, H * K))
            inp[f'bk{i}'] = jnp.zeros((H * K,), jnp.float32)
            inp[f'wv{i}'] = rn((D, H * K))
            inp[f'bv{i}'] = jnp.zeros((H * K,), jnp.float32)
            inp[f'wo{i}'] = rn((H * K, D))
            inp[f'bo{i}'] = jnp.zeros((D,), jnp.float32)
            inp[f'bias_k{i}'] = rn((1, 1, H, K))
            inp[f'bias_v{i}'] = rn((1, 1, H, K))
        inp['ln_mlp_scale'] = jnp.ones((D,), jnp.float32)
        inp['ln_mlp_offset'] = jnp.zeros((D,), jnp.float32)
        inp['w_fc1'] = rn((D, F))
        inp['b_fc1'] = jnp.zeros((F,), jnp.float32)
        inp['w_fc2'] = rn((F, D))
        inp['b_fc2'] = jnp.zeros((D,), jnp.float32)
        return inp
    _L1_xattn_all = _L1_xattn_setup()
    _L1_xattn_in = {k: v for k, v in _L1_xattn_all.items() if k in ('ln1_scale', 'ln1_offset', 'wq1', 'bq1', 'wk1', 'bk1', 'wv1', 'bv1', 'wo1', 'bo1', 'bias_k1', 'bias_v1', 'ln2_scale', 'ln2_offset', 'wq2', 'bq2', 'wk2', 'bk2', 'wv2', 'bv2', 'wo2', 'bo2', 'bias_k2', 'bias_v2', 'ln_mlp_scale', 'ln_mlp_offset', 'w_fc1', 'b_fc1', 'w_fc2', 'b_fc2')}
    del _L1_xattn_all
    return {'x': x, 'ctx_2048': ctx_2048, 'mask_Bx1xSxS2_ff0': mask_Bx1xSxS2_ff0, 'L0_xattn_Wq': _L0_xattn_in['Wq'], 'L0_xattn_bq': _L0_xattn_in['bq'], 'L0_xattn_Wk': _L0_xattn_in['Wk'], 'L0_xattn_bk': _L0_xattn_in['bk'], 'L0_xattn_Wv': _L0_xattn_in['Wv'], 'L0_xattn_bv': _L0_xattn_in['bv'], 'L0_xattn_Wo': _L0_xattn_in['Wo'], 'L0_xattn_bo': _L0_xattn_in['bo'], 'L0_xattn_gamma': _L0_xattn_in['gamma'], 'L0_xattn_beta': _L0_xattn_in['beta'], 'L1_xattn_ln1_scale': _L1_xattn_in['ln1_scale'], 'L1_xattn_ln1_offset': _L1_xattn_in['ln1_offset'], 'L1_xattn_wq1': _L1_xattn_in['wq1'], 'L1_xattn_bq1': _L1_xattn_in['bq1'], 'L1_xattn_wk1': _L1_xattn_in['wk1'], 'L1_xattn_bk1': _L1_xattn_in['bk1'], 'L1_xattn_wv1': _L1_xattn_in['wv1'], 'L1_xattn_bv1': _L1_xattn_in['bv1'], 'L1_xattn_wo1': _L1_xattn_in['wo1'], 'L1_xattn_bo1': _L1_xattn_in['bo1'], 'L1_xattn_bias_k1': _L1_xattn_in['bias_k1'], 'L1_xattn_bias_v1': _L1_xattn_in['bias_v1'], 'L1_xattn_ln2_scale': _L1_xattn_in['ln2_scale'], 'L1_xattn_ln2_offset': _L1_xattn_in['ln2_offset'], 'L1_xattn_wq2': _L1_xattn_in['wq2'], 'L1_xattn_bq2': _L1_xattn_in['bq2'], 'L1_xattn_wk2': _L1_xattn_in['wk2'], 'L1_xattn_bk2': _L1_xattn_in['bk2'], 'L1_xattn_wv2': _L1_xattn_in['wv2'], 'L1_xattn_bv2': _L1_xattn_in['bv2'], 'L1_xattn_wo2': _L1_xattn_in['wo2'], 'L1_xattn_bo2': _L1_xattn_in['bo2'], 'L1_xattn_bias_k2': _L1_xattn_in['bias_k2'], 'L1_xattn_bias_v2': _L1_xattn_in['bias_v2'], 'L1_xattn_ln_mlp_scale': _L1_xattn_in['ln_mlp_scale'], 'L1_xattn_ln_mlp_offset': _L1_xattn_in['ln_mlp_offset'], 'L1_xattn_w_fc1': _L1_xattn_in['w_fc1'], 'L1_xattn_b_fc1': _L1_xattn_in['b_fc1'], 'L1_xattn_w_fc2': _L1_xattn_in['w_fc2'], 'L1_xattn_b_fc2': _L1_xattn_in['b_fc2']}

def reference(x, ctx_2048, mask_Bx1xSxS2_ff0, L0_xattn_Wq, L0_xattn_bq, L0_xattn_Wk, L0_xattn_bk, L0_xattn_Wv, L0_xattn_bv, L0_xattn_Wo, L0_xattn_bo, L0_xattn_gamma, L0_xattn_beta, L1_xattn_ln1_scale, L1_xattn_ln1_offset, L1_xattn_wq1, L1_xattn_bq1, L1_xattn_wk1, L1_xattn_bk1, L1_xattn_wv1, L1_xattn_bv1, L1_xattn_wo1, L1_xattn_bo1, L1_xattn_bias_k1, L1_xattn_bias_v1, L1_xattn_ln2_scale, L1_xattn_ln2_offset, L1_xattn_wq2, L1_xattn_bq2, L1_xattn_wk2, L1_xattn_bk2, L1_xattn_wv2, L1_xattn_bv2, L1_xattn_wo2, L1_xattn_bo2, L1_xattn_bias_k2, L1_xattn_bias_v2, L1_xattn_ln_mlp_scale, L1_xattn_ln_mlp_offset, L1_xattn_w_fc1, L1_xattn_b_fc1, L1_xattn_w_fc2, L1_xattn_b_fc2):
    import jax
    import jax.numpy as jnp

    def _L0_xattn_ref(hidden_state, encoder_hidden_state, encoder_attention_mask, Wq, bq, Wk, bk, Wv, bv, Wo, bo, gamma, beta):
        import jax, jax.numpy as jnp
        import numpy as np
        H = 512
        NH = 32
        KVH = 8
        HD = H // NH
        GROUPS = NH // KVH
        EPS = 1e-06
        B, L, S = (4, 256, 256)

        def _gqa_forward(hidden_state, encoder_hidden_state, encoder_attention_mask, Wq, bq, Wk, bk, Wv, bv, Wo, bo, gamma, beta):
            b, l, _ = hidden_state.shape
            s = encoder_hidden_state.shape[1]
            q = hidden_state @ Wq + bq
            k = encoder_hidden_state @ Wk + bk
            v = encoder_hidden_state @ Wv + bv
            q = q.reshape(b, l, KVH, GROUPS, HD).transpose(0, 2, 3, 1, 4)
            k = k.reshape(b, s, KVH, HD).transpose(0, 2, 1, 3)
            v = v.reshape(b, s, KVH, HD).transpose(0, 2, 1, 3)
            scale = 1.0 / jnp.sqrt(jnp.asarray(HD, q.dtype))
            scores = jnp.einsum('bkgld,bksd->bkgls', q, k) * scale
            scores = scores + encoder_attention_mask[:, :, None, :, :]
            attn = jax.nn.softmax(scores, axis=-1)
            out = jnp.einsum('bkgls,bksd->bkgld', attn, v)
            out = out.transpose(0, 3, 1, 2, 4).reshape(b, l, H)
            out = out @ Wo + bo
            x = out + hidden_state
            mu = jnp.mean(x, axis=-1, keepdims=True)
            var = jnp.var(x, axis=-1, keepdims=True)
            return (x - mu) * jax.lax.rsqrt(var + EPS) * gamma + beta
        return _gqa_forward(hidden_state, encoder_hidden_state, encoder_attention_mask, Wq, bq, Wk, bk, Wv, bv, Wo, bo, gamma, beta)

    def _L1_xattn_ref(x, xf_1, xf_2, ln1_scale, ln1_offset, wq1, bq1, wk1, bk1, wv1, bv1, wo1, bo1, bias_k1, bias_v1, ln2_scale, ln2_offset, wq2, bq2, wk2, bk2, wv2, bv2, wo2, bo2, bias_k2, bias_v2, ln_mlp_scale, ln_mlp_offset, w_fc1, b_fc1, w_fc2, b_fc2):
        import jax, jax.numpy as jnp
        import numpy as np
        B, Q, S1, S2 = (4, 64, 512, 512)
        D, H, K, F = (512, 16, 128, 2048)
        LN_EPS = 1e-05

        def _layer_norm(x, scale, offset):
            mu = jnp.mean(x, axis=-1, keepdims=True)
            var = jnp.var(x, axis=-1, keepdims=True)
            return (x - mu) * jax.lax.rsqrt(var + LN_EPS) * scale + offset

        def _cross_attention(q_in, kv_in, wq, bq, wk, bk, wv, bv, wo, bo, bias_k, bias_v):
            b, q_len, _ = q_in.shape
            t = kv_in.shape[1]
            qh = (q_in @ wq + bq).reshape(b, q_len, H, K)
            kh = (kv_in @ wk + bk).reshape(b, t, H, K)
            vh = (kv_in @ wv + bv).reshape(b, t, H, K)
            kh = jnp.concatenate([kh, jnp.broadcast_to(bias_k, (b, 1, H, K))], axis=1)
            vh = jnp.concatenate([vh, jnp.broadcast_to(bias_v, (b, 1, H, K))], axis=1)
            scale = jnp.sqrt(jnp.asarray(K, q_in.dtype))
            logits = jnp.einsum('bqhk,bthk->bhqt', qh, kh) / scale
            weights = jax.nn.softmax(logits, axis=-1)
            ctx = jnp.einsum('bhqt,bthk->bqhk', weights, vh).reshape(b, q_len, H * K)
            return ctx @ wo + bo

        def _forward(x, xf_1, xf_2, ln1_scale, ln1_offset, wq1, bq1, wk1, bk1, wv1, bv1, wo1, bo1, bias_k1, bias_v1, ln2_scale, ln2_offset, wq2, bq2, wk2, bk2, wv2, bv2, wo2, bo2, bias_k2, bias_v2, ln_mlp_scale, ln_mlp_offset, w_fc1, b_fc1, w_fc2, b_fc2):
            res = x
            h = _layer_norm(x, ln1_scale, ln1_offset)
            x = res + _cross_attention(h, xf_1, wq1, bq1, wk1, bk1, wv1, bv1, wo1, bo1, bias_k1, bias_v1)
            res = x
            h = _layer_norm(x, ln2_scale, ln2_offset)
            x = res + _cross_attention(h, xf_2, wq2, bq2, wk2, bk2, wv2, bv2, wo2, bo2, bias_k2, bias_v2)
            h = _layer_norm(x, ln_mlp_scale, ln_mlp_offset)
            h = jax.nn.gelu(h @ w_fc1 + b_fc1, approximate=False) @ w_fc2 + b_fc2
            return x + h
        return _forward(x, xf_1, xf_2, ln1_scale, ln1_offset, wq1, bq1, wk1, bk1, wv1, bv1, wo1, bo1, bias_k1, bias_v1, ln2_scale, ln2_offset, wq2, bq2, wk2, bk2, wv2, bv2, wo2, bo2, bias_k2, bias_v2, ln_mlp_scale, ln_mlp_offset, w_fc1, b_fc1, w_fc2, b_fc2)
    x = _L0_xattn_ref(x, ctx_2048, mask_Bx1xSxS2_ff0, L0_xattn_Wq, L0_xattn_bq, L0_xattn_Wk, L0_xattn_bk, L0_xattn_Wv, L0_xattn_bv, L0_xattn_Wo, L0_xattn_bo, L0_xattn_gamma, L0_xattn_beta)
    x = _L1_xattn_ref(x, ctx_2048, ctx_2048, L1_xattn_ln1_scale, L1_xattn_ln1_offset, L1_xattn_wq1, L1_xattn_bq1, L1_xattn_wk1, L1_xattn_bk1, L1_xattn_wv1, L1_xattn_bv1, L1_xattn_wo1, L1_xattn_bo1, L1_xattn_bias_k1, L1_xattn_bias_v1, L1_xattn_ln2_scale, L1_xattn_ln2_offset, L1_xattn_wq2, L1_xattn_bq2, L1_xattn_wk2, L1_xattn_bk2, L1_xattn_wv2, L1_xattn_bv2, L1_xattn_wo2, L1_xattn_bo2, L1_xattn_bias_k2, L1_xattn_bias_v2, L1_xattn_ln_mlp_scale, L1_xattn_ln_mlp_offset, L1_xattn_w_fc1, L1_xattn_b_fc1, L1_xattn_w_fc2, L1_xattn_b_fc2)
    return x

_drawn_inputs = setup_inputs


def setup_inputs(seed=0):
    import zlib

    import numpy as np

    out = dict(_drawn_inputs(seed))
    spreads = {'L0_xattn_bq': (0.0, 0.8),
     'L0_xattn_bk': (0.0, 2.0),
     'L0_xattn_bv': (0.0, 0.1),
     'L0_xattn_bo': (0.0, 0.1),
     'L0_xattn_gamma': (1.0, 0.2),
     'L0_xattn_beta': (0.0, 0.1),
     'L1_xattn_ln1_scale': (1.0, 0.6),
     'L1_xattn_ln1_offset': (0.0, 0.8),
     'L1_xattn_bq1': (0.0, 0.8),
     'L1_xattn_bk1': (0.0, 2.0),
     'L1_xattn_bv1': (0.0, 0.1),
     'L1_xattn_bo1': (0.0, 0.1),
     'L1_xattn_ln2_scale': (1.0, 0.6),
     'L1_xattn_ln2_offset': (0.0, 0.8),
     'L1_xattn_bq2': (0.0, 0.8),
     'L1_xattn_bk2': (0.0, 2.0),
     'L1_xattn_bv2': (0.0, 0.1),
     'L1_xattn_bo2': (0.0, 0.1),
     'L1_xattn_ln_mlp_scale': (1.0, 0.2),
     'L1_xattn_ln_mlp_offset': (0.0, 0.361),
     'L1_xattn_b_fc1': (0.0, 0.1),
     'L1_xattn_b_fc2': (0.0, 0.1)}
    factors = {'L0_xattn_Wq': 7.77,
     'L0_xattn_Wk': 7.556,
     'L1_xattn_wq1': 3.815,
     'L1_xattn_wk1': 3.72,
     'L1_xattn_bias_k1': 64.0,
     'L1_xattn_bias_v1': 64.0,
     'L1_xattn_wq2': 3.834,
     'L1_xattn_wk2': 3.736,
     'L1_xattn_bias_k2': 64.0,
     'L1_xattn_bias_v2': 64.0}
    for name, (base, spread) in spreads.items():
        noise = np.random.default_rng([zlib.crc32(name.encode()), seed]).standard_normal(out[name].shape)
        drawn = base * np.exp(spread * noise) if base else spread * noise
        out[name] = jnp.asarray(drawn.astype(out[name].dtype))
    for name, factor in factors.items():
        out[name] = (out[name] * factor).astype(out[name].dtype)
    return out
```

```python
from contextlib import ExitStack

import concourse.bass as bass
from concourse import mybir

P = 128
F32 = mybir.dt.float32
F32R = mybir.dt.float32r
ALU = mybir.AluOpType
ACT = mybir.ActivationFunctionType
AXX = mybir.AxisListType.X

PASSES = ((0, 0), (0, 1), (1, 0))

D = 512
C = D // P
HALVES = 2
SEQ = 8
TB = 2
BT = SEQ // TB
BTOK = BT * P

NH0, HD0 = 32, 16
G0 = 2
UNITS0 = 2 * TB * G0
STEPS0 = UNITS0 * BT
VW = HD0 + 1
LAYERS = 2
H1, K1 = 16, 128
G1 = H1 // 2
T1 = P + 1
NB1 = G1 * TB
FG = 8

Q_SLABS = G0 + LAYERS * G1 + FG // 2
V_SLABS = 1 + LAYERS * G1 + FG // 2

COL_BQ0, COL_BK0, COL_BV0, COL_EVEN, COL_ODD = 0, 4, 8, 12, 13
COL_MLP_SCALE, COL_MLP_OFF, COL_FC1 = 14, 18, 22
COL_LAYER = 38
COL_BQ, COL_BK, COL_BIASK, COL_BIASV, COL_SCALE, COL_OFF = 0, 16, 32, 48, 64, 68
LAYER_COLS = 72
COLS = COL_LAYER + LAYERS * LAYER_COLS


def build(nc, x, xT, cT, mask, wq, wk, wv0, wv, wo, vec, ident_in, gb_rows, bo_rows, bv_rows, biasv_rows, out):
    ctx = ExitStack()
    with ctx:
        def sb(name, shape, dt=F32):
            return ctx.enter_context(nc.sbuf_tensor(name, shape, dt))

        def sem(name):
            return ctx.enter_context(nc.semaphore(name))

        X = sb("X", [P, SEQ, D])
        CT = sb("CT", [P, 2, C, SEQ * P], F32R)
        AT = sb("AT", [P, 2, C, SEQ * P], F32R)
        W = sb("W", [P, 4, 2, 1024], F32R)
        RAW = sb("RAW", [P, 4, 1024])
        XN = sb("XN", [P, BT, D])
        HF = sb("HF", [P, 2, BTOK])
        BVR = sb("BVR", [P, 2048])
        BIASVR = sb("BIASVR", [P, 2048])
        BO = sb("BO", [P, D])
        VEC = sb("VEC", [P, COLS])
        BQS = sb("BQS", [P, 4 + LAYERS * H1])
        IDENT = sb("IDENT", [P, P])
        BNS = sb("BNS", [P, BT, 6])
        MV = sb("MV", [P, BT, 2])
        SD = sb("SD", [P, BT])
        RS = sb("RS", [P, BT])
        NT = sb("NT", [P, BT])
        MX = sb("MX", [P, 3, 8])
        RC = sb("RC", [P, 2, 8])
        SUM = sb("SUM", [P, BT])

        ARENA = 43008
        at = (nc.sbuf_base + 31) // 32 * 32
        sb("arena", [P, ARENA // 4])

        def in_arena(name, shape, dt, offset):
            n = 4
            for s in shape[1:]:
                n *= s
            assert offset % 32 == 0 and offset + n <= ARENA, (name, offset, n)
            return nc.alloc_sbuf_tensor_at(name, shape, dt, offset=at + offset)

        Q0 = in_arena("Q0", [P, 2, BTOK], F32, 0)
        KZ = in_arena("KZ", [P, 2, BT, 2 * P], F32, 4096)
        P0 = in_arena("P0", [P, 3, 8 * P], F32, 12288)
        PT0 = in_arena("PT0", [P, 8 * P], F32, 24576)
        V0 = in_arena("V0", [P, SEQ, 8, VW], F32, 28672)
        CQ = in_arena("CQ", [P, 2, P], F32, 33024)
        CX0 = in_arena("CX0", [P, 2, 2, BTOK], F32R, 34048)
        Q = in_arena("Q", [P, BTOK], F32, 0)
        K = in_arena("K", [P, BT, 132], F32, 2048)
        V = in_arena("V", [P, 2, BT, 256], F32, 4160)
        PR = in_arena("PR", [P, BT, 132], F32, 12352)
        PT = in_arena("PT", [P, BTOK], F32, 14464)
        CX = in_arena("CX", [P, 2, 2, BTOK], F32R, 16512)
        HB = in_arena("HB", [P, 2, 2, 2, BTOK], F32R, 0)

        PS = ctx.enter_context(nc.psum_tensor("PS", [P, 8, 512], F32))
        BA, BB, BC, BD, BS, BPT, BPV = 0, 1, 2, 3, 4, 6, 7

        ld_const, ld_x, ld_rows, ld_bo, ld_src = sem("ld_const"), sem("ld_x"), sem("ld_rows"), sem("ld_bo"), sem("ld_src")
        ld = [sem(f"ld_{k}") for k in "qkvo"]
        w_hi = [sem(f"w_{k}_hi") for k in "qkvo"]
        w_ready = [sem(f"w_{k}_ready") for k in "qkvo"]
        src_hi, src_lo = sem("src_hi"), sem("src_lo")
        const_done = sem("const_done")
        ones_done = sem("ones_done")
        out_done = sem("out_done")
        v0_ps, v0_ev, q0_ps, q0_ev, k0_ps, k0_ev = (sem(n) for n in ("v0_ps", "v0_ev", "q0_ps", "q0_ev", "k0_ps", "k0_ev"))
        s0_ps, z0, max0, sub0, exp0 = (sem(n) for n in ("s0_ps", "z0", "max0", "sub0", "exp0"))
        t0_ps, t0_ev, pv0_ps, rc0, cq0 = (sem(n) for n in ("t0_ps", "t0_ev", "pv0_ps", "rc0", "cq0"))
        ct0_ps, cx0_hi, cx0_lo, o0_ps, xadd0 = (sem(n) for n in ("ct0_ps", "cx0_hi", "cx0_lo", "o0_ps", "xadd0"))
        ln_step, sd_done = sem("ln_step"), sem("sd_done")
        xn_done, free_done, tr_ps, f_done, at_hi, at_lo = (sem(n) for n in ("xn_done", "free_done", "tr_ps", "f_done", "at_hi", "at_lo"))
        bo_added, vb_done = sem("bo_added"), sem("vb_done")
        q_ps, q_ev, k_ps, k_ev, v_ps, v_ev = (sem(n) for n in ("q_ps", "q_ev", "k_ps", "k_ev", "v_ps", "v_ev"))
        s_ps, max_done, exp_done, rc_done, norm_done = (sem(n) for n in ("s_ps", "max_done", "exp_done", "rc_done", "norm_done"))
        t_ps, t_ev, pv_ps, cx_hi, cx_lo, o_ps, xadd = (sem(n) for n in ("t_ps", "t_ev", "pv_ps", "cx_hi", "cx_lo", "o_ps", "xadd"))
        h_ps, gelu_done, h_hi, h_lo, m_ps, madd = (sem(n) for n in ("h_ps", "gelu_done", "h_hi", "h_lo", "m_ps", "madd"))

        waited = sem("waited")

        block = ctx.enter_context(nc.Block())

        def slab3(t, n):
            return t.rearrange("p (c n) -> p c n", n=n)

        def norm_index(hf, ly):
            return hf * (LAYERS + 1) + ly

        def half_units(hf, ly):
            return (hf * LAYERS + ly) * NB1

        def take_wait(eng):
            eng.sem_inc(waited, 1)

        @block.sync
        def _(sp):
            sp.dma_start(VEC[:], vec).then_inc(ld_const, 16)
            sp.dma_start(IDENT[:], ident_in).then_inc(ld_const, 16)
            with sp.Fori(0, HALVES, 1) as hf:
                nq, nv = hf * Q_SLABS, hf * V_SLABS
                for i in range(2 * TB):
                    src, tb = (cT, xT)[i % 2], i // 2
                    sp.wait_ge(src_lo, hf * 4 + i)
                    sp.dma_start(XN[:], src[bass.ds(hf, 1), tb].rearrange("a p c t -> (a p) c t")).then_inc(ld_src, 16)
                    if i == 0:
                        sp.wait_ge(out_done, hf * 16)
                        take_wait(sp)
                        for n, raw in ((2, 2), (0, 0), (1, 1), (3, 3)):
                            s = hf * (V_SLABS if n == 2 else Q_SLABS)
                            sp.wait_ge(w_ready[n], s)
                            if n == 2:
                                sp.dma_start(RAW[:, 2, 0:512], wv0).then_inc(ld[2], 16)
                            else:
                                sp.dma_start(RAW[:, n, :], (wq, wk, None, wo)[n][0]).then_inc(ld[n], 16)
                        sp.dma_start(BIASVR[:, 0:SEQ * P].rearrange("p (b t) -> p b t", b=SEQ),
                                     mask[bass.ds(hf, 1)].rearrange("a p b t -> (a p) b t")).then_inc(ld_rows, 16)
                        sp.dma_start(BVR[:, 0:2 * D], gb_rows.to_broadcast([P, 2 * D])).then_inc(ld_rows, 16)
                        sp.dma_start(BO[:], bo_rows[0:1, :].to_broadcast([P, D])).then_inc(ld_bo, 16)
                        sp.dma_start(X[:], x[bass.ds(hf, 1)].rearrange("a b p n -> p (a b) n")).then_inc(ld_x, 16)
                for n in (0, 1, 3):
                    sp.wait_ge(w_ready[n], nq + 1)
                    sp.dma_start(RAW[:, n, :], (wq, wk, None, wo)[n][1]).then_inc(ld[n], 16)
                with sp.Fori(0, LAYERS, 1) as ly:
                    sp.wait_ge(free_done, hf * TB + TB)
                    sp.wait_ge(v_ev, half_units(hf, ly) * 2)
                    sp.dma_start(BVR[:], bv_rows[bass.ds(ly, 1), :].to_broadcast([P, 2048])).then_inc(ld_rows, 16)
                    sp.dma_start(BIASVR[:], biasv_rows[bass.ds(ly, 1), :].to_broadcast([P, 2048])).then_inc(ld_rows, 16)
                    sp.wait_ge(bo_added, (hf * 4 + ly + 1) * TB)
                    sp.dma_start(BO[:], bo_rows[bass.ds(ly + 1, 1), :].to_broadcast([P, D])).then_inc(ld_bo, 16)
                    with sp.Fori(0, G1, 1) as g:
                        for n in range(4):
                            s = ly * G1 + g + (0 if n == 2 else G0)
                            done = s + (nv + 1 if n == 2 else nq)
                            sp.wait_ge(w_ready[n], done)
                            sp.dma_start(RAW[:, n, :], (wq, wk, wv, wo)[n][bass.ds(s, 1)].rearrange("a p n -> (a p) n")).then_inc(ld[n], 16)
                sp.wait_ge(bo_added, (hf * 4 + 3) * TB)
                sp.dma_start(BO[:], bo_rows[3:4, :].to_broadcast([P, D])).then_inc(ld_bo, 16)
                with sp.Fori(0, FG // 2, 1) as gp:
                    for n in range(4):
                        s = gp + LAYERS * G1 + (0 if n == 2 else G0)
                        done = s + (nv + 1 if n == 2 else nq)
                        sp.wait_ge(w_ready[n], done)
                        sp.dma_start(RAW[:, n, :], (wq, wk, wv, wo)[n][bass.ds(s, 1)].rearrange("a p n -> (a p) n")).then_inc(ld[n], 16)
                sp.wait_ge(madd, (hf + 1) * FG * TB * BT)
                sp.dma_start(out[bass.ds(hf, 1)].rearrange("a b p n -> p (a b) n"), X[:]).then_inc(out_done, 16)
            sp.wait_ge(out_done, HALVES * 16)

        def split(eng, hi_op, n, count, width=1024):
            eng.wait_ge(ld[n], count * 16 + 16)
            take_wait(eng)
            hi_op(W[:, n, 0, 0:width], RAW[:, n, 0:width]).then_inc(w_hi[n], 1)
            eng.wait_ge(w_hi[n], count + 1)
            eng.tensor_tensor(W[:, n, 1, 0:width], RAW[:, n, 0:width],
                              W[:, n, 0, 0:width].bitcast(F32), ALU.subtract).then_inc(w_ready[n], 1)

        @block.gpsimd
        def _(pool):
            def copy_hi(out, in_):
                return nc.gpsimd.tensor_scalar(out, in_, 1.0, 0.0, ALU.mult, ALU.add)

            def psplit(n, count, width=1024):
                split(nc.gpsimd, copy_hi, n, count, width)

            def add_bo(tb):
                nc.gpsimd.tensor_tensor(X[:, tb * BT:(tb + 1) * BT, :], X[:, tb * BT:(tb + 1) * BT, :],
                                        BO[:].unsqueeze(1).to_broadcast([P, BT, D]), ALU.add).then_inc(bo_added, 1)

            with pool.Fori(0, HALVES, 1) as hf:
                nq, nv = hf * Q_SLABS, hf * V_SLABS
                psplit(2, nv, 512)
                psplit(0, nq)
                psplit(3, nq)
                nc.gpsimd.memset(V0[:, :, :, HD0:VW].rearrange("p b k o -> p (b k) o"), 1.0).then_inc(ones_done, 1)
                pool.wait_ge(ld_bo, hf * 64 + 16)
                pool.wait_ge(ld_x, hf * 16 + 16)
                for tb in range(TB):
                    add_bo(tb)
                for s in range(STEPS0):
                    pool.wait_ge(max0, hf * STEPS0 + (s + 1))
                    z = P0[:, s % 3, :].rearrange("p (h t) -> p h t", t=P)
                    nc.gpsimd.tensor_tensor(z, z, MX[:, s % 3, :].unsqueeze(2).to_broadcast([P, 8, P]),
                                            ALU.subtract).then_inc(sub0, 1)
                    if s == 10:
                        pool.wait_ge(q0_ps, hf * UNITS0 + 4)
                        psplit(0, nq + 1)
                    if s == 18:
                        pool.wait_ge(o0_ps, hf * 16 + 8)
                        psplit(3, nq + 1)
                with pool.Fori(0, LAYERS, 1) as ly:
                    b0 = half_units(hf, ly)
                    lq, lv = nq + G0 + ly * G1, nv + 1 + ly * G1
                    pool.wait_ge(xn_done, norm_index(hf, ly) * TB + 1)
                    psplit(0, lq)
                    psplit(2, lv)
                    pool.wait_ge(ld_bo, (hf * 4 + ly) * 16 + 32)
                    for tb in range(TB):
                        pool.wait_ge(xn_done, norm_index(hf, ly) * TB + (tb + 1))
                        add_bo(tb)

                    def body(g, first, last):
                        for tb in range(TB):
                            n = b0 + g * TB + tb
                            for h in range(2):
                                pool.wait_ge(rc_done, n * 2 + (h + 1))
                                nc.gpsimd.tensor_tensor(PR[:, :, 0:P], PR[:, :, 0:P],
                                                        RC[:, 0, 0:BT].unsqueeze(2).to_broadcast([P, BT, P]),
                                                        ALU.mult).then_inc(norm_done, 1)
                                if h == 0 and tb == 0:
                                    if not first:
                                        pool.wait_ge(o_ps, n * BT)
                                    psplit(3, lq + g)
                                if h == 0 and tb == 1 and not last:
                                    pool.wait_ge(q_ps, n * 2 + 2)
                                    psplit(0, lq + g + 1)
                                    psplit(2, lv + g + 1)

                    body(0, True, False)
                    with pool.Fori(1, G1 - 1, 1) as g:
                        body(g, False, False)
                    body(G1 - 1, False, True)
                lq, lv = nq + G0 + LAYERS * G1, nv + 1 + LAYERS * G1
                pool.wait_ge(xn_done, norm_index(hf, LAYERS) * TB + 1)
                for n in (0, 2, 1, 3):
                    psplit(n, lv if n == 2 else lq)
                pool.wait_ge(ld_bo, hf * 64 + 64)
                for tb in range(TB):
                    pool.wait_ge(xn_done, norm_index(hf, LAYERS) * TB + (tb + 1))
                    add_bo(tb)
                with pool.Fori(1, FG // 2, 1) as gp:
                    before = hf * FG * TB + gp * 4 - 4
                    for n in (0, 2, 1, 3):
                        if n < 2:
                            pool.wait_ge(h_ps, before * 2 + (4, 8)[n])
                        else:
                            pool.wait_ge(m_ps, before * BT + (8, 16)[n - 2])
                        psplit(n, (lv if n == 2 else lq) + gp)

        @block.tensor
        def _(pe):
            def triple(out, lhs, rhs, chunks, inc=None, first=True, last=True):
                k, total = 0, chunks * len(PASSES)
                for c in range(chunks):
                    for a, b in PASSES:
                        ins = nc.tensor.matmul(out, lhs(c, a), rhs(c, b), start=(k == 0), stop=(k == total - 1))
                        k += 1
                return ins

            def project(bank, kind, width, col, src, tb, done):
                w = W[:, kind].rearrange("p a (c n) -> p a c n", n=width)
                triple(PS[:, bank, :], lambda c, a: w[:, a, c, col:col + P],
                       lambda c, b: src[:, b, c, tb * BTOK:(tb + 1) * BTOK], C).then_inc(done, 1)

            pe.wait_ge(ld_const, 32)
            with pe.Fori(0, HALVES, 1) as hf:
                nq, nv = hf * Q_SLABS, hf * V_SLABS
                u0, s0, o0 = hf * UNITS0, hf * STEPS0, hf * 16

                def v0(tb):
                    pe.wait_ge(src_lo, hf * 4 + (2 * tb + 1))
                    pe.wait_ge(w_ready[2], nv + 1)
                    if tb:
                        pe.wait_ge(k0_ev, u0 + 2)
                    w = W[:, 2, :, 0:C * P].rearrange("p a (c n) -> p a c n", n=P)
                    for b in range(BT):
                        t = (tb * BT + b) * P
                        ins = triple(PS[:, BA, b * P:(b + 1) * P], lambda c, a: CT[:, a, c, t:t + P],
                                     lambda c, b_: w[:, b_, c, :], C)
                    ins.then_inc(v0_ps, 1)

                def qk0(u):
                    g, tb, j = u // 4, u // 2 % 2, u % 2
                    if j == 0:
                        if g == 0:
                            pe.wait_ge(src_lo, hf * 4 + (2 * tb + 2))
                            pe.wait_ge(v0_ev, hf * 2 + (tb + 1))
                        else:
                            pe.wait_ge(k0_ev, u0 + u)
                        pe.wait_ge(w_ready[0], nq + (g + 1))
                        pe.wait_ge(w_ready[1], nq + (g + 1))
                    elif u == 1:
                        pe.wait_ge(k0_ev, u0 + u)
                    else:
                        pe.wait_ge(xadd0, o0 + (u // 2) * BT)
                    project(BA, 0, 256, j * P, AT, tb, q0_ps)
                    pe.wait_ge(q0_ev, u0 + (u + 1))
                    project(BA, 1, 256, j * P, CT, tb, k0_ps)

                def s0_(s):
                    u, b = s // 4, s % 4
                    pe.wait_ge(q0_ev, u0 + (u + 1))
                    pe.wait_ge(k0_ev, u0 + (u + 1))
                    if s:
                        pe.wait_ge(z0, s0 + s)
                    for i in range(4):
                        rows = slice(32 * i, 32 * i + 32)
                        ins = nc.tensor.matmul(PS[:, BC + i, 0:2 * P], Q0[rows, u % 2, b * P:(b + 1) * P],
                                               KZ[rows, u % 2, b, :], start=True, stop=True)
                    ins.then_inc(s0_ps, 1)

                def ct0(s):
                    pe.wait_ge(cq0, s0 + (s + 1))
                    nc.tensor.transpose(PS[:, BB, 2 * P:3 * P], CQ[:, s % 2, :], IDENT[:]).then_inc(ct0_ps, 1)

                def t0(s):
                    pe.wait_ge(exp0, s0 + (s + 1))
                    if s:
                        pe.wait_ge(t0_ev, s0 + s)
                    for h in range(8):
                        ins = nc.tensor.transpose(PS[:, BPT + h // 4, h % 4 * P:(h % 4 + 1) * P],
                                                  P0[:, s % 3, h * P:(h + 1) * P], IDENT[:])
                    ins.then_inc(t0_ps, 1)

                def pv0(s):
                    u, b = s // 4, s % 4
                    g, tb, j = u // 4, u // 2 % 2, u % 2
                    pe.wait_ge(t0_ev, s0 + (s + 1))
                    if s == 0:
                        pe.wait_ge(v0_ev, hf * 2 + 1)
                        pe.wait_ge(ones_done, hf + 1)
                    else:
                        pe.wait_ge(cx0_lo, s0 + s)
                    for h in range(8):
                        kv = 2 * (2 * g + j) + h // 4
                        ins = nc.tensor.matmul(PS[:, BB, h * VW:(h + 1) * VW], PT0[:, h * P:(h + 1) * P],
                                               V0[:, tb * BT + b, kv, :], start=True, stop=True)
                    ins.then_inc(pv0_ps, 1)

                def out0(n):
                    pe.wait_ge(cx0_lo, s0 + (n + 1) * 8)
                    pe.wait_ge(w_ready[3], nq + (n // 2 + 1))
                    w = W[:, 3].rearrange("p a (h n) -> p a h n", n=D)
                    for t in range(BT):
                        if t == 0:
                            pe.wait_ge(k0_ev, u0 + min(2 * n + 3, UNITS0))
                        else:
                            pe.wait_ge(xadd0, o0 + (n * BT + t))
                        triple(PS[:, BA, :], lambda h, a: CX0[:, h, a, t * P:(t + 1) * P],
                               lambda h, b: w[:, b, h, :], 2).then_inc(o0_ps, 1)

                v0(0)
                qk0(0)
                s0_(0)
                s0_(1)
                for s in range(STEPS0):
                    u, b = s // 4, s % 4
                    if s + 2 < STEPS0:
                        s0_(s + 2)
                    if s:
                        ct0(s - 1)
                    t0(s)
                    pv0(s)
                    if s % 8 == 0 and s:
                        out0(s // 8 - 1)
                    if b == 1 and u + 1 < UNITS0:
                        if u == 1:
                            v0(1)
                        qk0(u + 1)
                ct0(STEPS0 - 1)
                out0(3)

                def norm_t(i):
                    for tb in range(TB):
                        t = i * TB + tb
                        pe.wait_ge(xn_done, t + 1)
                        for c in range(C):
                            if tb:
                                pe.wait_ge(f_done, t * C + (c - 3))
                            for b in range(BT):
                                ins = nc.tensor.transpose(PS[:, c, b * P:(b + 1) * P],
                                                          XN[:, b, c * P:(c + 1) * P], IDENT[:])
                            ins.then_inc(tr_ps, 1)

                with pe.Fori(0, LAYERS, 1) as ly:
                    b0 = half_units(hf, ly)
                    lq, lv = nq + G0 + ly * G1, nv + 1 + ly * G1
                    norm_t(norm_index(hf, ly))
                    pe.wait_ge(at_lo, norm_index(hf, ly) * 8 + 8)

                    def qk(n, tb, h, slab):
                        if h == 0:
                            pe.wait_ge(w_ready[0], slab + 1)
                            pe.wait_ge(w_ready[1], slab + 1)
                        pe.wait_ge(q_ev, n * 2 + h)
                        project(BA, 0, 256, h * P, AT, tb, q_ps)
                        pe.wait_ge(k_ev, n * 2 + h)
                        project(BB, 1, 256, h * P, CT, tb, k_ps)

                    def values(n, tb, slab, first):
                        w = W[:, 2].rearrange("p a (c n) -> p a c n", n=256)
                        pe.wait_ge(w_ready[2], slab + 1)
                        for i in range(2):
                            if not first:
                                pe.wait_ge(xadd, n * BT + (i - 5))
                            for b in range(2):
                                t = (tb * BT + 2 * i + b) * P
                                ins = triple(PS[:, BC + i, b * 256:(b + 1) * 256], lambda c, a: CT[:, a, c, t:t + P],
                                             lambda c, b_: w[:, b_, c, :], C)
                            ins.then_inc(v_ps, 1)

                    def scores(n, h):
                        pe.wait_ge(q_ev, n * 2 + (h + 1))
                        pe.wait_ge(k_ev, n * 2 + (h + 1))
                        pe.wait_ge(exp_done, n * 2 + h)
                        for b in range(BT):
                            ins = nc.tensor.matmul(PS[:, BS + b // 2, b % 2 * 256:b % 2 * 256 + T1],
                                                   Q[:, b * P:(b + 1) * P], K[:, b, 0:T1], start=True, stop=True)
                        ins.then_inc(s_ps, 1)

                    def transposes(n, h):
                        pe.wait_ge(norm_done, n * 2 + (h + 1))
                        pe.wait_ge(t_ev, n * 2 + h)
                        for b in range(BT):
                            ins = nc.tensor.transpose(PS[:, BPT, b * P:(b + 1) * P], PR[:, b, 0:P], IDENT[:])
                        ins.then_inc(t_ps, 1)

                    def weigh(n, tb, h):
                        pe.wait_ge(t_ev, n * 2 + (h + 1))
                        pe.wait_ge(v_ev, n * 2 + 2)
                        pe.wait_ge(cx_lo, n * 2 + h)
                        for b in range(BT):
                            ins = nc.tensor.matmul(PS[:, BPV, b * P:(b + 1) * P], V[:, tb, b, h * P:(h + 1) * P],
                                                   PT[:, b * P:(b + 1) * P], start=True, stop=True)
                        ins.then_inc(pv_ps, 1)

                    def rows(n, slab, more):
                        w = W[:, 3].rearrange("p a (h n) -> p a h n", n=D)
                        pe.wait_ge(cx_lo, n * 2 + 2)
                        pe.wait_ge(w_ready[3], slab + 1)
                        for t in range(BT):
                            if t < 2:
                                pe.wait_ge(v_ev, n * 2 + (t + 1 + 2 * more))
                            else:
                                pe.wait_ge(xadd, n * BT + (t - 1))
                            triple(PS[:, BC + t % 2, :], lambda h, a: CX[:, h, a, t * P:(t + 1) * P],
                                   lambda h, b: w[:, b, h, :], 2).then_inc(o_ps, 1)

                    def body(g, first, last):
                        for tb in range(TB):
                            n = b0 + g * TB + tb
                            end = last and tb == 1
                            scores(n, 0)
                            qk(n, tb, 1, lq + g)
                            transposes(n, 0)
                            if not (first and tb == 0):
                                rows(n - 1, lq + g - (1 - tb), 1)
                            weigh(n, tb, 0)
                            scores(n, 1)
                            if not end:
                                qk(n + 1, 1 - tb, 0, lq + g + tb)
                            transposes(n, 1)
                            if not end:
                                values(n + 1, 1 - tb, lv + g + tb, first and tb == 0)
                            weigh(n, tb, 1)

                    qk(b0, 0, 0, lq)
                    values(b0, 0, lv, True)
                    body(0, True, False)
                    with pe.Fori(1, G1 - 1, 1) as g:
                        body(g, False, False)
                    body(G1 - 1, False, True)
                    rows(b0 + (NB1 - 1), lq + (G1 - 1), 0)

                lq, lv = nq + G0 + LAYERS * G1, nv + 1 + LAYERS * G1
                norm_t(norm_index(hf, LAYERS))
                pe.wait_ge(at_lo, norm_index(hf, LAYERS) * 8 + 8)
                take_wait(pe)
                with pe.Fori(0, FG // 2, 1) as gp:
                    m0 = hf * FG * TB + gp * 4

                    def hidden(m):
                        e, tb = m // 2, m % 2
                        pe.wait_ge(w_ready[e], lq + gp + 1)
                        for f in range(2):
                            if m == 0:
                                pe.wait_ge(gelu_done, m0 * 2)
                            else:
                                pe.wait_ge(gelu_done, m0 * 2 + (2 * m + f - 1))
                            project(BA + f, e, 256, f * P, AT, tb, h_ps)

                    def down(m):
                        e = m // 2
                        w = W[:, 2 + e].rearrange("p a (h n) -> p a h n", n=D)
                        pe.wait_ge(h_lo, m0 * 2 + (2 * m + 2))
                        pe.wait_ge(w_ready[2 + e], (lq if e else lv) + gp + 1)
                        for t in range(BT):
                            if m or t:
                                pe.wait_ge(madd, m0 * BT + (m * BT + t - 1))
                            else:
                                pe.wait_ge(madd, m0 * BT)
                            triple(PS[:, BC + t % 2, :], lambda f, a: HB[:, m % 2, f, a, t * P:(t + 1) * P],
                                   lambda f, b: w[:, b, f, :], 2).then_inc(m_ps, 1)

                    hidden(0)
                    for m in range(1, 4):
                        hidden(m)
                        down(m - 1)
                    down(3)

        @block.scalar
        def _(act):
            act.wait_ge(const_done, 2)
            with act.Fori(0, HALVES, 1) as hf:
                u0, s0 = hf * UNITS0, hf * STEPS0

                def src(i):
                    act.wait_ge(ld_src, (hf * 4 + i) * 16 + 16)
                    tb = i // 2
                    nc.scalar.activation((CT, AT)[i % 2][:, 0, :, tb * BTOK:(tb + 1) * BTOK], XN[:], ACT.Copy).then_inc(src_hi, 1)

                def qev0(u):
                    act.wait_ge(q0_ps, u0 + (u + 1))
                    jj = u // 4 * 2 + u % 2
                    nc.scalar.activation(Q0[:, u % 2, :], PS[:, BA, :], ACT.Identity,
                                         bias=BQS[:, jj:jj + 1], scale=HD0 ** -0.5).then_inc(q0_ev, 1)

                def e0(s):
                    act.wait_ge(sub0, s0 + (s + 1))
                    nc.scalar.activation(P0[:, s % 3, :], P0[:, s % 3, :], ACT.Exp).then_inc(exp0, 1)

                def cxhi0(s):
                    u, b = s // 4, s % 4
                    jj = u // 4 * 2 + u % 2
                    act.wait_ge(ct0_ps, s0 + (s + 1))
                    nc.scalar.activation(CX0[:, u % 2, 0, b * P:(b + 1) * P], PS[:, BB, 2 * P:3 * P], ACT.Identity,
                                         bias=VEC[:, COL_BV0 + jj:COL_BV0 + jj + 1]).then_inc(cx0_hi, 1)

                src(0)
                src(1)
                qev0(0)
                src(2)
                e0(0)
                src(3)
                for s in range(STEPS0):
                    u, b = s // 4, s % 4
                    if s + 1 < STEPS0:
                        e0(s + 1)
                    if s:
                        cxhi0(s - 1)
                    act.wait_ge(t0_ps, s0 + (s + 1))
                    nc.scalar.activation(PT0[:].rearrange("p (a n) -> p a n", a=2), PS[:, BPT:BPT + 2, :],
                                         ACT.Copy).then_inc(t0_ev, 1)
                    if b == 1 and u + 1 < UNITS0:
                        qev0(u + 1)
                cxhi0(STEPS0 - 1)

                def root(r):
                    act.wait_ge(ln_step, r * 8 + 3)
                    nc.scalar.activation(SD[:], NT[:], ACT.Sqrt).then_inc(sd_done, 1)

                def norm(hf, i):
                    for tb in range(TB):
                        root((hf * 4 + (i + 1)) * 2 + tb)
                        t = norm_index(hf, i) * TB + tb
                        for c in range(C):
                            act.wait_ge(f_done, t * C + (c + 1))
                            nc.scalar.activation(AT[:, 0, c, tb * BTOK:(tb + 1) * BTOK], HF[:, c % 2, :], ACT.Copy).then_inc(at_hi, 1)

                root(hf * 8)
                root(hf * 8 + 1)
                with act.Fori(0, LAYERS, 1) as ly:
                    b0 = half_units(hf, ly)
                    norm(hf, ly)

                    def qev(n, h, head):
                        act.wait_ge(q_ps, n * 2 + (h + 1))
                        take_wait(act)
                        nc.scalar.activation(Q[:], PS[:, BA, :], ACT.Identity,
                                             bias=BQS[:, bass.ds(ly * H1 + head + 4, 1)], scale=K1 ** -0.5).then_inc(q_ev, 1)

                    def body(g, first, last):
                        for tb in range(TB):
                            n = b0 + g * TB + tb
                            for h in range(2):
                                act.wait_ge(max_done, n * 2 + (h + 1))
                                for b in range(BT):
                                    ins = nc.scalar.activation(PR[:, b, 0:T1], PS[:, BS + b // 2, b % 2 * 256:b % 2 * 256 + T1],
                                                               ACT.Exp, bias=MX[:, 0, b:b + 1], accum_out=SUM[:, b:b + 1])
                                ins.then_inc(exp_done, 1)
                                if h == 0:
                                    qev(n, 1, g * 2 + 1)
                                elif not (last and tb == 1):
                                    qev(n + 1, 0, g * 2 + 2 * tb)
                                act.wait_ge(t_ps, n * 2 + (h + 1))
                                nc.scalar.activation(PT[:], PS[:, BPT, :], ACT.Copy).then_inc(t_ev, 1)
                                act.wait_ge(pv_ps, n * 2 + (h + 1))
                                take_wait(act)
                                nc.scalar.activation(CX[:, h, 0, :], PS[:, BPV, :], ACT.Identity,
                                                     bias=VEC[:, bass.ds(ly * LAYER_COLS + g * 2 + (COL_LAYER + COL_BIASV + h), 1)]).then_inc(cx_hi, 1)

                    qev(b0, 0, 0)
                    body(0, True, False)
                    with act.Fori(1, G1 - 1, 1) as g:
                        body(g, False, False)
                    body(G1 - 1, False, True)
                norm(hf, LAYERS)
                with act.Fori(0, FG // 2, 1) as gp:
                    m0 = hf * FG * TB + gp * 4
                    for m in range(4):
                        for f in range(2):
                            act.wait_ge(h_ps, m0 * 2 + (2 * m + f + 1))
                            if m == 0:
                                act.wait_ge(h_lo, m0 * 2)
                            else:
                                act.wait_ge(h_lo, m0 * 2 + (2 * m + f - 1))
                            take_wait(act)
                            nc.scalar.activation(HF[:, f, :], PS[:, BA + f, :], ACT.Gelu,
                                                 bias=VEC[:, bass.ds(gp * 4 + (COL_FC1 + m // 2 * 2 + f), 1)]).then_inc(gelu_done, 1)

        @block.vector
        def _(dve):
            V_ = nc.vector
            dve.wait_ge(ld_const, 32)
            V_.tensor_scalar(BQS[:, 0:4], VEC[:, COL_BQ0:COL_BQ0 + 4], HD0 ** -0.5, None, ALU.mult).then_inc(const_done, 1)
            V_.tensor_scalar(BQS[:, 4:4 + LAYERS * H1].rearrange("p (l h) -> p l h", l=LAYERS),
                             VEC[:, COL_LAYER:COLS].rearrange("p (l n) -> p l n", l=LAYERS)[:, :, COL_BQ:COL_BQ + H1],
                             K1 ** -0.5, None, ALU.mult).then_inc(const_done, 1)

            def vsplit(n, count):
                split(V_, V_.tensor_copy, n, count)

            with dve.Fori(0, HALVES, 1) as hf:
                nq = hf * Q_SLABS
                u0, s0, o0 = hf * UNITS0, hf * STEPS0, hf * 16

                def src(i):
                    dve.wait_ge(src_hi, hf * 4 + (i + 1))
                    tb = i // 2
                    t = (CT, AT)[i % 2]
                    V_.tensor_tensor(t[:, 1, :, tb * BTOK:(tb + 1) * BTOK], XN[:],
                                     t[:, 0, :, tb * BTOK:(tb + 1) * BTOK].bitcast(F32), ALU.subtract).then_inc(src_lo, 1)

                def vev0(tb):
                    dve.wait_ge(v0_ps, hf * 2 + (tb + 1))
                    V_.tensor_copy(V0[:, tb * BT:(tb + 1) * BT, :, 0:HD0].rearrange("p b k d -> p (b k) d"),
                                   PS[:, BA, :].rearrange("p (k d) -> p k d", d=HD0)).then_inc(v0_ev, 1)

                def kev0(u):
                    jj = u // 4 * 2 + u % 2
                    dve.wait_ge(k0_ps, u0 + (u + 1))
                    for e in range(2):
                        ins = V_.tensor_scalar(KZ[:, u % 2, :, e * P:(e + 1) * P], PS[:, BA, :].rearrange("p (b t) -> p b t", t=P),
                                               VEC[:, COL_BK0 + jj:COL_BK0 + jj + 1],
                                               VEC[:, COL_EVEN + e:COL_EVEN + e + 1], ALU.add, ALU.mult)
                    ins.then_inc(k0_ev, 1)

                def soft0(s):
                    u, b = s // 4, s % 4
                    tile = u // 2 % 2 * BT + b
                    dve.wait_ge(s0_ps, s0 + (s + 1))
                    V_.tensor_tensor(P0[:, s % 3, :].rearrange("p (i e t) -> p i e t", e=2, t=P),
                                     PS[:, BC:BC + 4, 0:2 * P].rearrange("p i (e t) -> p i e t", e=2),
                                     BIASVR[:, tile * P:(tile + 1) * P].unsqueeze(1).unsqueeze(1).to_broadcast([P, 4, 2, P]),
                                     ALU.add).then_inc(z0, 1)
                    dve.wait_ge(z0, s0 + (s + 1))
                    V_.tensor_reduce(MX[:, s % 3, :], P0[:, s % 3, :].rearrange("p (h t) -> p h t", t=P),
                                     AXX, ALU.max).then_inc(max0, 1)

                def cxlo0(s):
                    u, b = s // 4, s % 4
                    jj = u // 4 * 2 + u % 2
                    dve.wait_ge(cx0_hi, s0 + (s + 1))
                    V_.scalar_tensor_tensor(CX0[:, u % 2, 1, b * P:(b + 1) * P], PS[:, BB, 2 * P:3 * P],
                                            VEC[:, COL_BV0 + jj:COL_BV0 + jj + 1],
                                            CX0[:, u % 2, 0, b * P:(b + 1) * P].bitcast(F32), ALU.add, ALU.subtract).then_inc(cx0_lo, 1)

                def cqs0(s):
                    dve.wait_ge(pv0_ps, s0 + (s + 1))
                    pv = PS[:, BB, 0:8 * VW].rearrange("p (h d) -> p h d", d=VW)
                    V_.reciprocal(RC[:, s % 2, :].unsqueeze(2), pv[:, :, HD0:VW]).then_inc(rc0, 1)
                    dve.wait_ge(rc0, s0 + (s + 1))
                    V_.tensor_tensor(CQ[:, s % 2, :].rearrange("p (h d) -> p h d", d=HD0), pv[:, :, 0:HD0],
                                     RC[:, s % 2, :].unsqueeze(2).to_broadcast([P, 8, HD0]), ALU.mult).then_inc(cq0, 1)

                def add_rows(bank, tile, filled, count, done):
                    dve.wait_ge(filled, count)
                    V_.tensor_tensor(X[:, tile, :], PS[:, bank, :], X[:, tile, :], ALU.add).then_inc(done, 1)

                def add0(n):
                    for t in range(BT):
                        add_rows(BA, n % 2 * BT + t, o0_ps, o0 + (n * BT + t + 1), xadd0)

                src(0)
                vsplit(1, nq)
                src(1)
                dve.wait_ge(ld_rows, hf * 96 + 32)
                vev0(0)
                kev0(0)
                src(2)
                soft0(0)
                soft0(1)
                src(3)
                dve.wait_ge(bo_added, hf * 8 + 2)
                for s in range(STEPS0):
                    u, b = s // 4, s % 4
                    if s + 2 < STEPS0:
                        soft0(s + 2)
                    if s:
                        cxlo0(s - 1)
                    cqs0(s)
                    if s % 8 == 0 and s:
                        add0(s // 8 - 1)
                    if s == 10:
                        vsplit(1, nq + 1)
                    if b == 1 and u + 1 < UNITS0:
                        if u == 1:
                            vev0(1)
                        kev0(u + 1)
                cxlo0(STEPS0 - 1)
                add0(3)

                def step(r, k, ins):
                    ins.then_inc(ln_step, 1)
                    dve.wait_ge(ln_step, r * 8 + k)

                def norm_x(r, tb, eps):
                    for b in range(BT):
                        ins = V_.bn_stats(BNS[:, b, :], X[:, tb * BT + b, :])
                    step(r, 1, ins)
                    take_wait(dve)
                    for b in range(BT):
                        ins = V_.bn_aggr(MV[:, b, :], BNS[:, b, :])
                    step(r, 2, ins)
                    V_.tensor_scalar(NT[:], MV[:, :, 1], eps, None, ALU.add).then_inc(ln_step, 1)
                    dve.wait_ge(sd_done, r + 1)
                    step(r, 4, V_.reciprocal(RS[:], SD[:]))
                    step(r, 5, V_.tensor_tensor(SUM[:], RS[:], RS[:], ALU.mult))
                    step(r, 6, V_.tensor_tensor(NT[:], NT[:], SUM[:], ALU.mult))
                    step(r, 7, V_.tensor_scalar(NT[:], NT[:], -0.5, 1.5, ALU.mult, ALU.add))
                    step(r, 8, V_.tensor_tensor(RS[:], RS[:], NT[:], ALU.mult))
                    for b in range(BT):
                        ins = V_.tensor_scalar(XN[:, b, :], X[:, tb * BT + b, :], MV[:, b, 0:1], RS[:, b:b + 1],
                                               ALU.subtract, ALU.mult)
                    return ins

                def norm(hf, i, eps, scale_col, off_col):
                    for tb in range(TB):
                        t = norm_index(hf, i) * TB + tb
                        dve.wait_ge(tr_ps, t * C)
                        norm_x((hf * 4 + (i + 1)) * 2 + tb, tb, eps).then_inc(xn_done, 1)

                        def low(c):
                            dve.wait_ge(at_hi, t * C + (c + 1))
                            V_.tensor_tensor(AT[:, 1, c, tb * BTOK:(tb + 1) * BTOK], HF[:, c % 2, :],
                                             AT[:, 0, c, tb * BTOK:(tb + 1) * BTOK].bitcast(F32), ALU.subtract).then_inc(at_lo, 1)

                        for c in range(C):
                            if c >= 2:
                                low(c - 2)
                                dve.wait_ge(at_lo, t * C + (c - 1))
                            dve.wait_ge(tr_ps, t * C + (c + 1))
                            V_.tensor_scalar(HF[:, c % 2, :], PS[:, c, :], VEC[:, bass.ds(scale_col + c, 1)],
                                             VEC[:, bass.ds(off_col + c, 1)], ALU.mult, ALU.add).then_inc(f_done, 1)
                        low(2)
                        low(3)

                dve.wait_ge(xadd0, o0 + 16)
                for tb in range(TB):
                    if tb:
                        dve.wait_ge(free_done, hf * 2 + 1)
                    ins = norm_x(hf * 8 + tb, tb, 1e-6)
                    ins.then_inc(vb_done, 1)
                    dve.wait_ge(vb_done, hf * 6 + (2 * tb + 1))
                    V_.tensor_tensor(XN[:], XN[:], BVR[:, 0:D].unsqueeze(1).to_broadcast([P, BT, D]), ALU.mult).then_inc(vb_done, 1)
                    dve.wait_ge(vb_done, hf * 6 + (2 * tb + 2))
                    V_.tensor_tensor(X[:, tb * BT:(tb + 1) * BT, :], XN[:], BVR[:, D:2 * D].unsqueeze(1).to_broadcast([P, BT, D]),
                                     ALU.add).then_inc(free_done, 1)
                dve.wait_ge(free_done, hf * 2 + 2)
                take_wait(dve)

                with dve.Fori(0, LAYERS, 1) as ly:
                    b0 = half_units(hf, ly)
                    lq = nq + G0 + ly * G1
                    cols = ly * LAYER_COLS + COL_LAYER
                    dve.wait_ge(xadd, b0 * BT)
                    norm(hf, ly, 1e-5, cols + COL_SCALE, cols + COL_OFF)
                    vsplit(1, lq)
                    dve.wait_ge(ld_rows, (hf * 6 + ly * 2) * 16 + 64)
                    V_.tensor_tensor(BVR[:], BVR[:], BIASVR[:], ALU.subtract).then_inc(vb_done, 1)
                    dve.wait_ge(vb_done, hf * 6 + ly + 5)

                    def kev(n, h, head):
                        V_.tensor_copy(K[:, :, P:T1], VEC[:, bass.ds(cols + head + COL_BIASK, 1)].unsqueeze(1).to_broadcast([P, BT, 1]))
                        dve.wait_ge(k_ps, n * 2 + (h + 1))
                        V_.tensor_scalar(K[:, :, 0:P], PS[:, BB, :].rearrange("p (b t) -> p b t", t=P),
                                         VEC[:, bass.ds(cols + head + COL_BK, 1)], None, ALU.add).then_inc(k_ev, 1)

                    def vev(n, tb, g):
                        for i in range(2):
                            dve.wait_ge(v_ps, n * 2 + (i + 1))
                            V_.tensor_tensor(V[:, tb, 2 * i:2 * i + 2, :], PS[:, BC + i, :].rearrange("p (b d) -> p b d", d=256),
                                             BVR[:, bass.ds(g * 256, 256)].unsqueeze(1).to_broadcast([P, 2, 256]),
                                             ALU.add).then_inc(v_ev, 1)

                    def soft(n, h):
                        dve.wait_ge(s_ps, n * 2 + (h + 1))
                        V_.tensor_reduce(MX[:, 0, 0:BT].rearrange("p (a b) -> p a b", a=2),
                                         PS[:, BS:BS + 2, :].rearrange("p a (b t) -> p a b t", b=2)[:, :, :, 0:T1],
                                         AXX, ALU.max, negate=True).then_inc(max_done, 1)
                        dve.wait_ge(exp_done, n * 2 + (h + 1))
                        V_.reciprocal(RC[:, 0, 0:BT], SUM[:]).then_inc(rc_done, 1)

                    def body(g, first, last):
                        for tb in range(TB):
                            n = b0 + g * TB + tb
                            end = last and tb == 1
                            for h in range(2):
                                soft(n, h)
                                if h == 0:
                                    kev(n, 1, g * 2 + 1)
                                    if tb == 1 and not last:
                                        vsplit(1, lq + g + 1)
                                    if not (first and tb == 0):
                                        for t in range(BT):
                                            add_rows(BC + t % 2, (1 - tb) * BT + t, o_ps, n * BT + (t - BT + 1), xadd)
                                elif not end:
                                    kev(n + 1, 0, g * 2 + 2 * tb)
                                    vev(n + 1, 1 - tb, g + tb)
                                dve.wait_ge(cx_hi, n * 2 + (h + 1))
                                V_.scalar_tensor_tensor(CX[:, h, 1, :], PS[:, BPV, :],
                                                        VEC[:, bass.ds(cols + g * 2 + (COL_BIASV + h), 1)],
                                                        CX[:, h, 0, :].bitcast(F32), ALU.add, ALU.subtract).then_inc(cx_lo, 1)

                    kev(b0, 0, 0)
                    vev(b0, 0, 0)
                    body(0, True, False)
                    with dve.Fori(1, G1 - 1, 1) as g:
                        body(g, False, False)
                    body(G1 - 1, False, True)
                    for t in range(BT):
                        add_rows(BC + t % 2, BT + t, o_ps, (b0 + (NB1 - 1)) * BT + (t + 1), xadd)

                dve.wait_ge(xadd, half_units(hf, LAYERS) * BT)
                norm(hf, LAYERS, 1e-5, COL_MLP_SCALE, COL_MLP_OFF)
                dve.wait_ge(bo_added, hf * 8 + 8)
                take_wait(dve)
                with dve.Fori(0, FG // 2, 1) as gp:
                    m0 = hf * FG * TB + gp * 4

                    def hsplit(m):
                        for f in range(2):
                            dve.wait_ge(gelu_done, m0 * 2 + (2 * m + f + 1))
                            V_.tensor_copy(HB[:, m % 2, f, 0, :], HF[:, f, :]).then_inc(h_hi, 1)
                            dve.wait_ge(h_hi, m0 * 2 + (2 * m + f + 1))
                            V_.tensor_tensor(HB[:, m % 2, f, 1, :], HF[:, f, :], HB[:, m % 2, f, 0, :].bitcast(F32),
                                             ALU.subtract).then_inc(h_lo, 1)

                    def madd_(m):
                        for t in range(BT):
                            add_rows(BC + t % 2, m % 2 * BT + t, m_ps, m0 * BT + (m * BT + t + 1), madd)

                    hsplit(0)
                    for m in range(1, 4):
                        hsplit(m)
                        madd_(m - 1)
                    madd_(3)


def _slabs(np, w, n):
    k, cols = w.shape
    return w.reshape(k // P, P, cols // n, n).transpose(2, 1, 0, 3).reshape(cols // n, P, k // P * n)


def _row_slabs(np, w):
    return w.reshape(-1, 2, P, D).transpose(0, 2, 1, 3).reshape(-1, P, 2 * D)


def _layout(np, a):
    halves = lambda x: x.reshape(HALVES, TB, BT, P, C, P).transpose(0, 1, 5, 4, 2, 3).reshape(HALVES, TB, P, C, BTOK)
    kv_cols = np.arange(NH0 * HD0) // 64 * HD0 + np.arange(NH0 * HD0) % HD0
    pair = lambda n: (a[f"L1_xattn_{n}1"], a[f"L1_xattn_{n}2"])
    w1, w2 = _slabs(np, a["L1_xattn_w_fc1"], 256), _row_slabs(np, a["L1_xattn_w_fc2"])
    per = lambda v: v.reshape(-1, P).T
    odd = (np.arange(P) // HD0 % 2).astype(np.float32)
    cols = [per(a["L0_xattn_bq"]), per(a["L0_xattn_bk"][kv_cols]), per(a["L0_xattn_bv"][kv_cols]),
            (np.float32(1) - odd)[:, None], odd[:, None], per(a["L1_xattn_ln_mlp_scale"]),
            per(a["L1_xattn_ln_mlp_offset"]), per(a["L1_xattn_b_fc1"])]
    for i in (1, 2):
        cols += [per(a[f"L1_xattn_{n}{i}"]) for n in ("bq", "bk", "bias_k", "bias_v")]
        cols += [per(a[f"L1_xattn_ln{i}_{n}"]) for n in ("scale", "offset")]
    return {
        "x": a["x"].reshape(HALVES, SEQ, P, D),
        "xT": halves(a["x"]),
        "cT": halves(a["ctx_2048"]),
        "mask": a["mask_Bx1xSxS2_ff0"].reshape(HALVES, SEQ, P, P).transpose(0, 2, 1, 3),
        "wq": np.concatenate([_slabs(np, a["L0_xattn_Wq"], 256)] + [_slabs(np, w, 256) for w in pair("wq")] + [w1[0::2]]),
        "wk": np.concatenate([_slabs(np, a["L0_xattn_Wk"][:, kv_cols], 256)] + [_slabs(np, w, 256) for w in pair("wk")] + [w1[1::2]]),
        "wv0": _slabs(np, a["L0_xattn_Wv"], P)[0],
        "wv": np.concatenate([_slabs(np, w, 256) for w in pair("wv")] + [w2[0::2]]),
        "wo": np.concatenate([_row_slabs(np, a["L0_xattn_Wo"])] + [_row_slabs(np, w) for w in pair("wo")] + [w2[1::2]]),
        "vec": np.concatenate(cols, axis=1),
        "ident": np.eye(P, dtype=np.float32),
        "gb_rows": np.concatenate([a["L0_xattn_gamma"], a["L0_xattn_beta"]])[None],
        "bo_rows": np.stack([a["L0_xattn_bo"], a["L1_xattn_bo1"], a["L1_xattn_bo2"], a["L1_xattn_b_fc2"]]),
        "bv_rows": np.stack(pair("bv")),
        "biasv_rows": np.stack([v.reshape(-1) for v in pair("bias_v")]),
    }


def kernel(**inputs):
    import numpy as np
    import concourse.bacc as bacc
    from concourse.bass_utils import run_bass_kernel_spmd

    laid = _layout(np, {k: np.asarray(v) for k, v in inputs.items()})
    nc = bacc.Bacc("TRN2", target_bir_lowering=False, num_devices=1)
    arrays, args = {}, []
    for name, a in laid.items():
        a = np.ascontiguousarray(a)
        arrays[f"in_{name}"] = a
        args.append(nc.dram_tensor(f"in_{name}", a.shape, mybir.dt.from_np(a.dtype), kind="ExternalInput").ap())
    args.append(nc.dram_tensor("out_0", (HALVES, SEQ, P, D), F32, kind="ExternalOutput").ap())
    build(nc, *args)
    r = run_bass_kernel_spmd(nc, [arrays], core_ids=[0])
    return r.results[0]["out_0"].reshape(HALVES * SEQ, P, D)
```

```python
from contextlib import ExitStack

import concourse.bass as bass
from concourse import mybir

P = 128
F32 = mybir.dt.float32
F32R = mybir.dt.float32r
ALU = mybir.AluOpType
ACT = mybir.ActivationFunctionType
AXX = mybir.AxisListType.X

PASSES = ((0, 0), (0, 1), (1, 0))

D = 512
C = D // P
HALVES = 2
SEQ = 8
TB = 2
BT = SEQ // TB
BTOK = BT * P

NH0, HD0 = 32, 16
G0 = 2
UNITS0 = 2 * TB * G0
STEPS0 = UNITS0 * BT
LAYERS = 2
H1, K1 = 16, 128
G1 = H1 // 2
T1 = P + 1
NB1 = G1 * TB
FG = 8

Q_SLABS = G0 + LAYERS * G1 + FG // 2
V_SLABS = 1 + LAYERS * G1 + FG // 2

COL_BQ0, COL_BK0, COL_BV0, COL_EVEN, COL_ODD = 0, 4, 8, 12, 13
COL_MLP_SCALE, COL_MLP_OFF, COL_FC1 = 14, 18, 22
COL_LAYER = 38
COL_BQ, COL_BK, COL_BIASK, COL_BIASV, COL_SCALE, COL_OFF = 0, 16, 32, 48, 64, 68
LAYER_COLS = 72
COLS = COL_LAYER + LAYERS * LAYER_COLS


def build(nc, x, xT, cT, mask, wq, wk, wv0, wv, wo, vec, ident_in, gb_rows, bo_rows, bv_rows, biasv_rows, out):
    ctx = ExitStack()
    with ctx:
        def sb(name, shape, dt=F32):
            return ctx.enter_context(nc.sbuf_tensor(name, shape, dt))

        def sem(name):
            return ctx.enter_context(nc.semaphore(name))

        X = sb("X", [P, SEQ, D])
        CT = sb("CT", [P, 2, C, SEQ * P], F32R)
        AT = sb("AT", [P, 2, C, SEQ * P], F32R)
        W = sb("W", [P, 4, 2, 1024], F32R)
        RAW = sb("RAW", [P, 4, 1024])
        XN = sb("XN", [P, BT, D])
        HF = sb("HF", [P, 2, BTOK])
        BVR = sb("BVR", [P, 2048])
        BIASVR = sb("BIASVR", [P, 2048])
        BO = sb("BO", [P, D])
        VEC = sb("VEC", [P, COLS])
        BKM = sb("BKM", [P, 2, 4])
        BQS = sb("BQS", [P, 4 + LAYERS * H1])
        IDENT = sb("IDENT", [P, P])
        BNS = sb("BNS", [P, BT, 6])
        MV = sb("MV", [P, BT, 2])
        SD = sb("SD", [P, BT])
        RS = sb("RS", [P, BT])
        NT = sb("NT", [P, BT])
        MX = sb("MX", [P, 3, 8])
        RC = sb("RC", [P, 2, 8])
        SUM = sb("SUM", [P, BT])
        SUM0 = sb("SUM0", [P, 2, 8])

        ARENA = 43008
        at = (nc.sbuf_base + 31) // 32 * 32
        sb("arena", [P, ARENA // 4])

        def in_arena(name, shape, dt, offset):
            n = 4
            for s in shape[1:]:
                n *= s
            assert offset % 32 == 0 and offset + n <= ARENA, (name, offset, n)
            return nc.alloc_sbuf_tensor_at(name, shape, dt, offset=at + offset)

        KZ = in_arena("KZ", [P, BT, 8, P], F32, 0)
        VP = in_arena("VP", [P, 2, 8, P], F32, 16384)
        CX0 = in_arena("CX0", [P, 2, 2, BTOK], F32R, 24576)
        Q0 = in_arena("Q0", [P, BTOK], F32, 32768)
        V0 = in_arena("V0", [P, SEQ, 8, HD0], F32, 34816)
        PT0A = in_arena("PT0A", [P, 8 * P], F32, 38912)
        P0 = [XN[:, 0:2, :].rearrange("p a n -> p (a n)"), XN[:, 2:4, :].rearrange("p a n -> p (a n)"),
              HF[:].rearrange("p a n -> p (a n)")]
        PT0 = [PT0A[:], BVR[:, 1024:2048]]
        Q = in_arena("Q", [P, BTOK], F32, 0)
        K = in_arena("K", [P, BT, 132], F32, 2048)
        V = in_arena("V", [P, 2, BT, 256], F32, 4160)
        PR = in_arena("PR", [P, BT, 132], F32, 12352)
        PT = in_arena("PT", [P, BTOK], F32, 14464)
        CX = in_arena("CX", [P, 2, 2, BTOK], F32R, 16512)
        HB = in_arena("HB", [P, 2, 2, 2, BTOK], F32R, 0)

        STAGE = [XN[:], X[:, 0:BT, :], X[:, BT:SEQ, :], XN[:]]

        PS = ctx.enter_context(nc.psum_tensor("PS", [P, 8, 512], F32))
        BA, BB, BC, BD, BS, BPT, BPV = 0, 1, 2, 3, 4, 6, 7

        ld_const, ld_x, ld_rows, ld_bo = sem("ld_const"), sem("ld_x"), sem("ld_rows"), sem("ld_bo")
        ld_src = [sem(f"ld_src{i}") for i in range(3)]
        ld = [sem(f"ld_{k}") for k in "qkvo"]
        w_hi = [sem(f"w_{k}_hi") for k in "qkvo"]
        w_ready = [sem(f"w_{k}_ready") for k in "qkvo"]
        src_hi, src_lo = sem("src_hi"), sem("src_lo")
        const_done = sem("const_done")
        zeros_done = sem("zeros_done")
        out_done = sem("out_done")
        v0_ps, v0_ev, q0_ps, q0_ev, k0_ps, k0_ev = (sem(n) for n in ("v0_ps", "v0_ev", "q0_ps", "q0_ev", "k0_ps", "k0_ev"))
        k0_ev2 = sem("k0_ev2")
        s0_ps, z0, max0, exp0, rc0, norm0 = (sem(n) for n in ("s0_ps", "z0", "max0", "exp0", "rc0", "norm0"))
        t0_ps, t0_ev, pv0_ps, vp0 = (sem(n) for n in ("t0_ps", "t0_ev", "pv0_ps", "vp0"))
        cx0_hi, cx0_lo, o0_ps, xadd0 = (sem(n) for n in ("cx0_hi", "cx0_lo", "o0_ps", "xadd0"))
        ln_step, sd_done = sem("ln_step"), sem("sd_done")
        xn_done, free_done, tr_ps, f_done, at_hi, at_lo = (sem(n) for n in ("xn_done", "free_done", "tr_ps", "f_done", "at_hi", "at_lo"))
        bo_added, vb_done = sem("bo_added"), sem("vb_done")
        q_ps, q_ev, k_ps, k_ev, v_ps, v_ev = (sem(n) for n in ("q_ps", "q_ev", "k_ps", "k_ev", "v_ps", "v_ev"))
        s_ps, max_done, exp_done, rc_done, norm_done = (sem(n) for n in ("s_ps", "max_done", "exp_done", "rc_done", "norm_done"))
        t_ps, t_ev, pv_ps, cx_hi, cx_lo, o_ps, xadd = (sem(n) for n in ("t_ps", "t_ev", "pv_ps", "cx_hi", "cx_lo", "o_ps", "xadd"))
        h_ps, gelu_done, h_hi, h_lo, m_ps, madd = (sem(n) for n in ("h_ps", "gelu_done", "h_hi", "h_lo", "m_ps", "madd"))

        waited = sem("waited")

        block = ctx.enter_context(nc.Block())

        def slab3(t, n):
            return t.rearrange("p (c n) -> p c n", n=n)

        def norm_index(hf, ly):
            return hf * (LAYERS + 1) + ly

        def half_units(hf, ly):
            return (hf * LAYERS + ly) * NB1

        def take_wait(eng):
            eng.sem_inc(waited, 1)

        @block.sync
        def _(sp):
            sp.dma_start(VEC[:], vec).then_inc(ld_const, 16)
            sp.dma_start(IDENT[:], ident_in).then_inc(ld_const, 16)
            with sp.Fori(0, HALVES, 1) as hf:
                nq, nv = hf * Q_SLABS, hf * V_SLABS
                half = lambda t: t[bass.ds(hf, 1)]

                def load_src(i):
                    sp.dma_start(STAGE[i], half((cT, xT)[i % 2])[:, i // 2].rearrange("a p c t -> (a p) c t")).then_inc(ld_src[i % 3], 16)

                load_src(0)
                sp.wait_ge(out_done, hf * 16)
                take_wait(sp)
                load_src(1)
                for n in (2, 0, 1):
                    if n == 2:
                        sp.dma_start(RAW[:, 2, 0:512], wv0).then_inc(ld[2], 16)
                    else:
                        sp.dma_start(RAW[:, n, :], (wq, wk)[n][0]).then_inc(ld[n], 16)
                load_src(2)
                sp.dma_start(BIASVR[:, 0:SEQ * P].rearrange("p (b t) -> p b t", b=SEQ),
                             half(mask).rearrange("a p b t -> (a p) b t")).then_inc(ld_rows, 16)
                sp.wait_ge(src_lo, hf * 4 + 1)
                load_src(3)
                sp.dma_start(RAW[:, 3, :], wo[0]).then_inc(ld[3], 16)
                sp.dma_start(BVR[:, 0:2 * D], gb_rows.to_broadcast([P, 2 * D])).then_inc(ld_rows, 16)
                sp.dma_start(BO[:], bo_rows[0:1, :].to_broadcast([P, D])).then_inc(ld_bo, 16)
                sp.wait_ge(src_lo, hf * 4 + 3)
                sp.dma_start(X[:], half(x).rearrange("a b p n -> p (a b) n")).then_inc(ld_x, 16)
                for n in (0, 1, 3):
                    sp.wait_ge(w_ready[n], nq + 1)
                    sp.dma_start(RAW[:, n, :], (wq, wk, None, wo)[n][1]).then_inc(ld[n], 16)
                with sp.Fori(0, LAYERS, 1) as ly:
                    sp.wait_ge(free_done, hf * TB + TB)
                    sp.wait_ge(v_ev, half_units(hf, ly) * 2)
                    sp.dma_start(BVR[:], bv_rows[bass.ds(ly, 1), :].to_broadcast([P, 2048])).then_inc(ld_rows, 16)
                    sp.dma_start(BIASVR[:], biasv_rows[bass.ds(ly, 1), :].to_broadcast([P, 2048])).then_inc(ld_rows, 16)
                    sp.wait_ge(bo_added, (hf * 4 + ly + 1) * TB)
                    sp.dma_start(BO[:], bo_rows[bass.ds(ly + 1, 1), :].to_broadcast([P, D])).then_inc(ld_bo, 16)
                    with sp.Fori(0, G1, 1) as g:
                        for n in range(4):
                            s = ly * G1 + g + (0 if n == 2 else G0)
                            done = s + (nv + 1 if n == 2 else nq)
                            sp.wait_ge(w_ready[n], done)
                            sp.dma_start(RAW[:, n, :], (wq, wk, wv, wo)[n][bass.ds(s, 1)].rearrange("a p n -> (a p) n")).then_inc(ld[n], 16)
                sp.wait_ge(bo_added, (hf * 4 + 3) * TB)
                sp.dma_start(BO[:], bo_rows[3:4, :].to_broadcast([P, D])).then_inc(ld_bo, 16)
                with sp.Fori(0, FG // 2, 1) as gp:
                    for n in range(4):
                        s = gp + LAYERS * G1 + (0 if n == 2 else G0)
                        done = s + (nv + 1 if n == 2 else nq)
                        sp.wait_ge(w_ready[n], done)
                        sp.dma_start(RAW[:, n, :], (wq, wk, wv, wo)[n][bass.ds(s, 1)].rearrange("a p n -> (a p) n")).then_inc(ld[n], 16)
                sp.wait_ge(madd, (hf + 1) * FG * TB * BT)
                sp.dma_start(out[bass.ds(hf, 1)].rearrange("a b p n -> p (a b) n"), X[:]).then_inc(out_done, 16)
            sp.wait_ge(out_done, HALVES * 16)

        def split(eng, hi_op, n, count, width=1024):
            eng.wait_ge(ld[n], count * 16 + 16)
            take_wait(eng)
            hi_op(W[:, n, 0, 0:width], RAW[:, n, 0:width]).then_inc(w_hi[n], 1)
            eng.wait_ge(w_hi[n], count + 1)
            eng.tensor_tensor(W[:, n, 1, 0:width], RAW[:, n, 0:width],
                              W[:, n, 0, 0:width].bitcast(F32), ALU.subtract).then_inc(w_ready[n], 1)

        @block.gpsimd
        def _(pool):
            def copy_hi(out, in_):
                return nc.gpsimd.tensor_scalar(out, in_, 1.0, 0.0, ALU.mult, ALU.add)

            def psplit(n, count, width=1024):
                split(nc.gpsimd, copy_hi, n, count, width)

            def add_bo(tb):
                nc.gpsimd.tensor_tensor(X[:, tb * BT:(tb + 1) * BT, :], X[:, tb * BT:(tb + 1) * BT, :],
                                        BO[:].unsqueeze(1).to_broadcast([P, BT, D]), ALU.add).then_inc(bo_added, 1)

            with pool.Fori(0, HALVES, 1) as hf:
                nq, nv = hf * Q_SLABS, hf * V_SLABS
                psplit(2, nv, 512)
                psplit(0, nq)
                psplit(3, nq)
                pool.wait_ge(ld_bo, hf * 64 + 16)
                pool.wait_ge(ld_x, hf * 16 + 16)

                def norm(s):
                    pool.wait_ge(rc0, hf * STEPS0 + (s + 1))
                    z = P0[s % 3].rearrange("p (h t) -> p h t", t=P)
                    nc.gpsimd.tensor_tensor(z, z, RC[:, s % 2, :].unsqueeze(2).to_broadcast([P, 8, P]),
                                            ALU.mult).then_inc(norm0, 1)

                def pad(s):
                    u, b = s // 4, s % 4
                    jj = u // 4 * 2 + u % 2
                    if s == 0:
                        pool.wait_ge(v0_ev, hf * 2 + 1)
                        pool.wait_ge(zeros_done, hf * 2 + 2)
                    if s == 8:
                        pool.wait_ge(v0_ev, hf * 2 + 2)
                    if s >= 2:
                        pool.wait_ge(pv0_ps, hf * STEPS0 + (s - 1))
                    v = V0[:, u // 2 % 2 * BT + b, 2 * jj:2 * jj + 2, :]
                    take_wait(pool)
                    for h in range(8):
                        ins = nc.gpsimd.tensor_copy(VP[:, s % 2, h, h * HD0:(h + 1) * HD0], v[:, h // 4, :])
                    ins.then_inc(vp0, 1)

                for tb in range(TB):
                    add_bo(tb)
                norm(0)
                for s in range(STEPS0):
                    pad(s)
                    if s + 1 < STEPS0:
                        norm(s + 1)
                    if s == 10:
                        pool.wait_ge(q0_ps, hf * UNITS0 + 4)
                        psplit(0, nq + 1)
                    if s == 18:
                        pool.wait_ge(o0_ps, hf * 16 + 8)
                        psplit(3, nq + 1)
                with pool.Fori(0, LAYERS, 1) as ly:
                    b0 = half_units(hf, ly)
                    lq, lv = nq + G0 + ly * G1, nv + 1 + ly * G1
                    pool.wait_ge(xn_done, norm_index(hf, ly) * TB + 1)
                    psplit(0, lq)
                    psplit(2, lv)
                    pool.wait_ge(ld_bo, (hf * 4 + ly) * 16 + 32)
                    for tb in range(TB):
                        pool.wait_ge(xn_done, norm_index(hf, ly) * TB + (tb + 1))
                        add_bo(tb)

                    def body(g, first, last):
                        for tb in range(TB):
                            n = b0 + g * TB + tb
                            for h in range(2):
                                pool.wait_ge(rc_done, n * 2 + (h + 1))
                                nc.gpsimd.tensor_tensor(PR[:, :, 0:P], PR[:, :, 0:P],
                                                        RC[:, 0, 0:BT].unsqueeze(2).to_broadcast([P, BT, P]),
                                                        ALU.mult).then_inc(norm_done, 1)
                                if h == 0 and tb == 0:
                                    if not first:
                                        pool.wait_ge(o_ps, n * BT)
                                    psplit(3, lq + g)
                                if h == 0 and tb == 1 and not last:
                                    pool.wait_ge(q_ps, n * 2 + 2)
                                    psplit(0, lq + g + 1)
                                    psplit(2, lv + g + 1)

                    body(0, True, False)
                    with pool.Fori(1, G1 - 1, 1) as g:
                        body(g, False, False)
                    body(G1 - 1, False, True)
                lq, lv = nq + G0 + LAYERS * G1, nv + 1 + LAYERS * G1
                pool.wait_ge(xn_done, norm_index(hf, LAYERS) * TB + 1)
                for n in (0, 2, 1, 3):
                    psplit(n, lv if n == 2 else lq)
                pool.wait_ge(ld_bo, hf * 64 + 64)
                for tb in range(TB):
                    pool.wait_ge(xn_done, norm_index(hf, LAYERS) * TB + (tb + 1))
                    add_bo(tb)
                with pool.Fori(1, FG // 2, 1) as gp:
                    before = hf * FG * TB + gp * 4 - 4
                    for n in (0, 2, 1, 3):
                        if n < 2:
                            pool.wait_ge(h_ps, before * 2 + (4, 8)[n])
                        else:
                            pool.wait_ge(m_ps, before * BT + (8, 16)[n - 2])
                        psplit(n, (lv if n == 2 else lq) + gp)

        @block.tensor
        def _(pe):
            def triple(out, lhs, rhs, chunks, inc=None, first=True, last=True):
                k, total = 0, chunks * len(PASSES)
                for c in range(chunks):
                    for a, b in PASSES:
                        ins = nc.tensor.matmul(out, lhs(c, a), rhs(c, b), start=(k == 0), stop=(k == total - 1))
                        k += 1
                return ins

            def project(bank, kind, width, col, src, tb, done):
                w = W[:, kind].rearrange("p a (c n) -> p a c n", n=width)
                triple(PS[:, bank, :], lambda c, a: w[:, a, c, col:col + P],
                       lambda c, b: src[:, b, c, tb * BTOK:(tb + 1) * BTOK], C).then_inc(done, 1)

            pe.wait_ge(ld_const, 32)
            with pe.Fori(0, HALVES, 1) as hf:
                nq, nv = hf * Q_SLABS, hf * V_SLABS
                u0, s0, o0 = hf * UNITS0, hf * STEPS0, hf * 16

                def v0(tb):
                    pe.wait_ge(src_lo, hf * 4 + (2 * tb + 1))
                    pe.wait_ge(w_ready[2], nv + 1)
                    w = W[:, 2, :, 0:C * P].rearrange("p a (c n) -> p a c n", n=P)
                    for b in range(BT):
                        t = (tb * BT + b) * P
                        ins = triple(PS[:, BC + tb, b * P:(b + 1) * P], lambda c, a: CT[:, a, c, t:t + P],
                                     lambda c, b_: w[:, b_, c, :], C)
                    ins.then_inc(v0_ps, 1)

                def qk0(u):
                    g, tb, j = u // 4, u // 2 % 2, u % 2
                    if u < 4 and j == 0:
                        pe.wait_ge(src_lo, hf * 4 + (2 * tb + 2))
                    pe.wait_ge(w_ready[0], nq + (g + 1))
                    pe.wait_ge(w_ready[1], nq + (g + 1))
                    project(BA, 0, 256, j * P, AT, tb, q0_ps)
                    if u >= 2:
                        pe.wait_ge(cx0_lo, s0 + (4 * u - 4))
                    project(BB, 1, 256, j * P, CT, tb, k0_ps)

                def s0_(s):
                    u, b = s // 4, s % 4
                    pe.wait_ge(q0_ev, u0 + (u + 1))
                    pe.wait_ge(k0_ev, u0 + (u + 1))
                    pe.wait_ge(k0_ev2, u0 + (u + 1))
                    if s:
                        pe.wait_ge(z0, s0 + s)
                    for i in range(2):
                        ins = nc.tensor.matmul(PS[:, BS + i, :], Q0[:, b * P:(b + 1) * P],
                                               KZ[:, b, 4 * i:4 * i + 4, :], start=True, stop=True)
                    ins.then_inc(s0_ps, 1)

                def t0(s):
                    pe.wait_ge(norm0, s0 + (s + 1))
                    if s:
                        pe.wait_ge(t0_ev, s0 + s)
                    for h in range(8):
                        ins = nc.tensor.transpose(PS[:, BPT + h // 4, h % 4 * P:(h % 4 + 1) * P],
                                                  P0[s % 3][:, h * P:(h + 1) * P], IDENT[:])
                    ins.then_inc(t0_ps, 1)

                def pv0(s):
                    pe.wait_ge(t0_ev, s0 + (s + 1))
                    pe.wait_ge(vp0, s0 + (s + 1))
                    if s:
                        pe.wait_ge(cx0_lo, s0 + s)
                    if s % 4 == 0:
                        pe.wait_ge(k0_ev, u0 + min(s // 4 + 2, UNITS0) if s else u0 + 2)
                        pe.wait_ge(k0_ev2, u0 + min(s // 4 + 2, UNITS0) if s else u0 + 2)
                    for h in range(8):
                        ins = nc.tensor.matmul(PS[:, BB, 0:P], VP[:, s % 2, h, :], PT0[s % 2][:, h * P:(h + 1) * P],
                                               start=(h == 0), stop=(h == 7))
                    ins.then_inc(pv0_ps, 1)

                def out0(n):
                    pe.wait_ge(cx0_lo, s0 + (n + 1) * 8)
                    pe.wait_ge(w_ready[3], nq + (n // 2 + 1))
                    w = W[:, 3].rearrange("p a (h n) -> p a h n", n=D)
                    for t in range(BT):
                        if t >= 2:
                            pe.wait_ge(xadd0, o0 + (n * BT + t - 1))
                        elif n:
                            pe.wait_ge(xadd0, o0 + n * BT)
                        else:
                            pe.wait_ge(v0_ev, hf * 2 + (t + 1))
                        triple(PS[:, BC + t % 2, :], lambda h, a: CX0[:, h, a, t * P:(t + 1) * P],
                               lambda h, b: w[:, b, h, :], 2).then_inc(o0_ps, 1)

                v0(0)
                qk0(0)
                v0(1)
                s0_(0)
                s0_(1)
                for s in range(STEPS0):
                    u, b = s // 4, s % 4
                    if s + 2 < STEPS0:
                        s0_(s + 2)
                    if b == 1 and u + 1 < UNITS0:
                        qk0(u + 1)
                    t0(s)
                    if s % 8 == 1 and s > 1:
                        out0(s // 8 - 1)
                    if s:
                        pv0(s - 1)
                pv0(STEPS0 - 1)
                out0(3)

                def norm_t(i):
                    for tb in range(TB):
                        t = i * TB + tb
                        pe.wait_ge(xn_done, t + 1)
                        for c in range(C):
                            if tb:
                                pe.wait_ge(f_done, t * C + (c - 3))
                            for b in range(BT):
                                ins = nc.tensor.transpose(PS[:, c, b * P:(b + 1) * P],
                                                          XN[:, b, c * P:(c + 1) * P], IDENT[:])
                            ins.then_inc(tr_ps, 1)

                with pe.Fori(0, LAYERS, 1) as ly:
                    b0 = half_units(hf, ly)
                    lq, lv = nq + G0 + ly * G1, nv + 1 + ly * G1
                    norm_t(norm_index(hf, ly))
                    pe.wait_ge(at_lo, norm_index(hf, ly) * 8 + 8)

                    def qk(n, tb, h, slab):
                        if h == 0:
                            pe.wait_ge(w_ready[0], slab + 1)
                            pe.wait_ge(w_ready[1], slab + 1)
                        pe.wait_ge(q_ev, n * 2 + h)
                        project(BA, 0, 256, h * P, AT, tb, q_ps)
                        pe.wait_ge(k_ev, n * 2 + h)
                        project(BB, 1, 256, h * P, CT, tb, k_ps)

                    def values(n, tb, slab, first):
                        w = W[:, 2].rearrange("p a (c n) -> p a c n", n=256)
                        pe.wait_ge(w_ready[2], slab + 1)
                        for i in range(2):
                            if not first:
                                pe.wait_ge(xadd, n * BT + (i - 5))
                            for b in range(2):
                                t = (tb * BT + 2 * i + b) * P
                                ins = triple(PS[:, BC + i, b * 256:(b + 1) * 256], lambda c, a: CT[:, a, c, t:t + P],
                                             lambda c, b_: w[:, b_, c, :], C)
                            ins.then_inc(v_ps, 1)

                    def scores(n, h):
                        pe.wait_ge(q_ev, n * 2 + (h + 1))
                        pe.wait_ge(k_ev, n * 2 + (h + 1))
                        pe.wait_ge(exp_done, n * 2 + h)
                        for b in range(BT):
                            ins = nc.tensor.matmul(PS[:, BS + b // 2, b % 2 * 256:b % 2 * 256 + T1],
                                                   Q[:, b * P:(b + 1) * P], K[:, b, 0:T1], start=True, stop=True)
                        ins.then_inc(s_ps, 1)

                    def transposes(n, h):
                        pe.wait_ge(norm_done, n * 2 + (h + 1))
                        pe.wait_ge(t_ev, n * 2 + h)
                        for b in range(BT):
                            ins = nc.tensor.transpose(PS[:, BPT, b * P:(b + 1) * P], PR[:, b, 0:P], IDENT[:])
                        ins.then_inc(t_ps, 1)

                    def weigh(n, tb, h):
                        pe.wait_ge(t_ev, n * 2 + (h + 1))
                        pe.wait_ge(v_ev, n * 2 + 2)
                        pe.wait_ge(cx_lo, n * 2 + h)
                        for b in range(BT):
                            ins = nc.tensor.matmul(PS[:, BPV, b * P:(b + 1) * P], V[:, tb, b, h * P:(h + 1) * P],
                                                   PT[:, b * P:(b + 1) * P], start=True, stop=True)
                        ins.then_inc(pv_ps, 1)

                    def rows(n, slab, more):
                        w = W[:, 3].rearrange("p a (h n) -> p a h n", n=D)
                        pe.wait_ge(cx_lo, n * 2 + 2)
                        pe.wait_ge(w_ready[3], slab + 1)
                        for t in range(BT):
                            if t < 2:
                                pe.wait_ge(v_ev, n * 2 + (t + 1 + 2 * more))
                            else:
                                pe.wait_ge(xadd, n * BT + (t - 1))
                            triple(PS[:, BC + t % 2, :], lambda h, a: CX[:, h, a, t * P:(t + 1) * P],
                                   lambda h, b: w[:, b, h, :], 2).then_inc(o_ps, 1)

                    def body(g, first, last):
                        for tb in range(TB):
                            n = b0 + g * TB + tb
                            end = last and tb == 1
                            scores(n, 0)
                            qk(n, tb, 1, lq + g)
                            transposes(n, 0)
                            if not (first and tb == 0):
                                rows(n - 1, lq + g - (1 - tb), 1)
                            weigh(n, tb, 0)
                            scores(n, 1)
                            if not end:
                                qk(n + 1, 1 - tb, 0, lq + g + tb)
                            transposes(n, 1)
                            if not end:
                                values(n + 1, 1 - tb, lv + g + tb, first and tb == 0)
                            weigh(n, tb, 1)

                    qk(b0, 0, 0, lq)
                    values(b0, 0, lv, True)
                    body(0, True, False)
                    with pe.Fori(1, G1 - 1, 1) as g:
                        body(g, False, False)
                    body(G1 - 1, False, True)
                    rows(b0 + (NB1 - 1), lq + (G1 - 1), 0)

                lq, lv = nq + G0 + LAYERS * G1, nv + 1 + LAYERS * G1
                norm_t(norm_index(hf, LAYERS))
                pe.wait_ge(at_lo, norm_index(hf, LAYERS) * 8 + 8)
                take_wait(pe)
                with pe.Fori(0, FG // 2, 1) as gp:
                    m0 = hf * FG * TB + gp * 4

                    def hidden(m):
                        e, tb = m // 2, m % 2
                        pe.wait_ge(w_ready[e], lq + gp + 1)
                        for f in range(2):
                            if m == 0:
                                pe.wait_ge(gelu_done, m0 * 2)
                            else:
                                pe.wait_ge(gelu_done, m0 * 2 + (2 * m + f - 1))
                            project(BA + f, e, 256, f * P, AT, tb, h_ps)

                    def down(m):
                        e = m // 2
                        w = W[:, 2 + e].rearrange("p a (h n) -> p a h n", n=D)
                        pe.wait_ge(h_lo, m0 * 2 + (2 * m + 2))
                        pe.wait_ge(w_ready[2 + e], (lq if e else lv) + gp + 1)
                        for t in range(BT):
                            if m or t:
                                pe.wait_ge(madd, m0 * BT + (m * BT + t - 1))
                            else:
                                pe.wait_ge(madd, m0 * BT)
                            triple(PS[:, BC + t % 2, :], lambda f, a: HB[:, m % 2, f, a, t * P:(t + 1) * P],
                                   lambda f, b: w[:, b, f, :], 2).then_inc(m_ps, 1)

                    hidden(0)
                    for m in range(1, 4):
                        hidden(m)
                        down(m - 1)
                    down(3)

        @block.scalar
        def _(act):
            act.wait_ge(const_done, 4)
            with act.Fori(0, HALVES, 1) as hf:
                u0, s0 = hf * UNITS0, hf * STEPS0

                def src(i):
                    act.wait_ge(ld_src[i % 3], hf * (32 if i % 3 == 0 else 16) + (32 if i == 3 else 16))
                    tb = i // 2
                    nc.scalar.activation((CT, AT)[i % 2][:, 0, :, tb * BTOK:(tb + 1) * BTOK], STAGE[i], ACT.Copy).then_inc(src_hi, 1)

                def qkev0(u):
                    act.wait_ge(q0_ps, u0 + (u + 1))
                    jj = u // 4 * 2 + u % 2
                    nc.scalar.activation(Q0[:], PS[:, BA, :], ACT.Identity,
                                         bias=BQS[:, jj:jj + 1], scale=HD0 ** -0.5).then_inc(q0_ev, 1)
                    if u == 0:
                        act.wait_ge(zeros_done, hf * 2 + 1)
                    act.wait_ge(k0_ps, u0 + (u + 1))
                    for i in (2, 3):
                        rows = slice(32 * i, 32 * i + 32)
                        for e in range(2):
                            ins = nc.scalar.activation(KZ[rows, :, 2 * i + e, :], PS[rows, BB, :].rearrange("p (b t) -> p b t", t=P),
                                                       ACT.Identity, bias=BKM[rows, e, jj:jj + 1],
                                                       scale=VEC[rows, COL_EVEN + e:COL_EVEN + e + 1])
                    ins.then_inc(k0_ev2, 1)

                def e0(s):
                    act.wait_ge(max0, s0 + (s + 1))
                    if s >= 2:
                        act.wait_ge(rc0, s0 + (s - 1))
                    for h in range(8):
                        ins = nc.scalar.activation(P0[s % 3][:, h * P:(h + 1) * P], P0[s % 3][:, h * P:(h + 1) * P], ACT.Exp,
                                                   bias=MX[:, s % 3, h:h + 1], accum_out=SUM0[:, s % 2, h:h + 1])
                    ins.then_inc(exp0, 1)

                def cxhi0(s):
                    u, b = s // 4, s % 4
                    jj = u // 4 * 2 + u % 2
                    act.wait_ge(pv0_ps, s0 + (s + 1))
                    nc.scalar.activation(CX0[:, u % 2, 0, b * P:(b + 1) * P], PS[:, BB, 0:P], ACT.Identity,
                                         bias=VEC[:, COL_BV0 + jj:COL_BV0 + jj + 1]).then_inc(cx0_hi, 1)

                for i in range(4):
                    src(i)
                qkev0(0)
                e0(0)
                e0(1)
                for s in range(STEPS0):
                    u, b = s // 4, s % 4
                    if b == 1 and u + 1 < UNITS0:
                        qkev0(u + 1)
                    act.wait_ge(t0_ps, s0 + (s + 1))
                    nc.scalar.activation(PT0[s % 2].rearrange("p (a n) -> p a n", a=2), PS[:, BPT:BPT + 2, :],
                                         ACT.Copy).then_inc(t0_ev, 1)
                    if s + 2 < STEPS0:
                        e0(s + 2)
                    if s:
                        cxhi0(s - 1)
                cxhi0(STEPS0 - 1)

                def root(r):
                    act.wait_ge(ln_step, r * 8 + 3)
                    nc.scalar.activation(SD[:], NT[:], ACT.Sqrt).then_inc(sd_done, 1)

                def norm(hf, i):
                    for tb in range(TB):
                        root((hf * 4 + (i + 1)) * 2 + tb)
                        t = norm_index(hf, i) * TB + tb
                        for c in range(C):
                            act.wait_ge(f_done, t * C + (c + 1))
                            nc.scalar.activation(AT[:, 0, c, tb * BTOK:(tb + 1) * BTOK], HF[:, c % 2, :], ACT.Copy).then_inc(at_hi, 1)

                root(hf * 8)
                root(hf * 8 + 1)
                with act.Fori(0, LAYERS, 1) as ly:
                    b0 = half_units(hf, ly)
                    norm(hf, ly)

                    def qev(n, h, head):
                        act.wait_ge(q_ps, n * 2 + (h + 1))
                        take_wait(act)
                        nc.scalar.activation(Q[:], PS[:, BA, :], ACT.Identity,
                                             bias=BQS[:, bass.ds(ly * H1 + head + 4, 1)], scale=K1 ** -0.5).then_inc(q_ev, 1)

                    def body(g, first, last):
                        for tb in range(TB):
                            n = b0 + g * TB + tb
                            for h in range(2):
                                act.wait_ge(max_done, n * 2 + (h + 1))
                                for b in range(BT):
                                    ins = nc.scalar.activation(PR[:, b, 0:T1], PS[:, BS + b // 2, b % 2 * 256:b % 2 * 256 + T1],
                                                               ACT.Exp, bias=MX[:, 0, b:b + 1], accum_out=SUM[:, b:b + 1])
                                ins.then_inc(exp_done, 1)
                                if h == 0:
                                    qev(n, 1, g * 2 + 1)
                                elif not (last and tb == 1):
                                    qev(n + 1, 0, g * 2 + 2 * tb)
                                act.wait_ge(t_ps, n * 2 + (h + 1))
                                nc.scalar.activation(PT[:], PS[:, BPT, :], ACT.Copy).then_inc(t_ev, 1)
                                act.wait_ge(pv_ps, n * 2 + (h + 1))
                                take_wait(act)
                                nc.scalar.activation(CX[:, h, 0, :], PS[:, BPV, :], ACT.Identity,
                                                     bias=VEC[:, bass.ds(ly * LAYER_COLS + g * 2 + (COL_LAYER + COL_BIASV + h), 1)]).then_inc(cx_hi, 1)

                    qev(b0, 0, 0)
                    body(0, True, False)
                    with act.Fori(1, G1 - 1, 1) as g:
                        body(g, False, False)
                    body(G1 - 1, False, True)
                norm(hf, LAYERS)
                with act.Fori(0, FG // 2, 1) as gp:
                    m0 = hf * FG * TB + gp * 4
                    for m in range(4):
                        for f in range(2):
                            act.wait_ge(h_ps, m0 * 2 + (2 * m + f + 1))
                            if m == 0:
                                act.wait_ge(h_lo, m0 * 2)
                            else:
                                act.wait_ge(h_lo, m0 * 2 + (2 * m + f - 1))
                            take_wait(act)
                            nc.scalar.activation(HF[:, f, :], PS[:, BA + f, :], ACT.Gelu,
                                                 bias=VEC[:, bass.ds(gp * 4 + (COL_FC1 + m // 2 * 2 + f), 1)]).then_inc(gelu_done, 1)

        @block.vector
        def _(dve):
            V_ = nc.vector
            dve.wait_ge(ld_const, 32)
            V_.tensor_scalar(BQS[:, 0:4], VEC[:, COL_BQ0:COL_BQ0 + 4], HD0 ** -0.5, None, ALU.mult).then_inc(const_done, 1)
            V_.tensor_scalar(BQS[:, 4:4 + LAYERS * H1].rearrange("p (l h) -> p l h", l=LAYERS),
                             VEC[:, COL_LAYER:COLS].rearrange("p (l n) -> p l n", l=LAYERS)[:, :, COL_BQ:COL_BQ + H1],
                             K1 ** -0.5, None, ALU.mult).then_inc(const_done, 1)

            for e in range(2):
                V_.tensor_scalar(BKM[:, e, :], VEC[:, COL_BK0:COL_BK0 + 4], VEC[:, COL_EVEN + e:COL_EVEN + e + 1],
                                 None, ALU.mult).then_inc(const_done, 1)

            def vsplit(n, count):
                split(V_, V_.tensor_copy, n, count)

            with dve.Fori(0, HALVES, 1) as hf:
                nq = hf * Q_SLABS
                u0, s0, o0 = hf * UNITS0, hf * STEPS0, hf * 16

                def src(i):
                    dve.wait_ge(src_hi, hf * 4 + (i + 1))
                    tb = i // 2
                    t = (CT, AT)[i % 2]
                    V_.tensor_tensor(t[:, 1, :, tb * BTOK:(tb + 1) * BTOK], STAGE[i],
                                     t[:, 0, :, tb * BTOK:(tb + 1) * BTOK].bitcast(F32), ALU.subtract).then_inc(src_lo, 1)

                def vev0(tb):
                    dve.wait_ge(v0_ps, hf * 2 + (tb + 1))
                    V_.tensor_copy(V0[:, tb * BT:(tb + 1) * BT, :, :].rearrange("p b k d -> p (b k d)"),
                                   PS[:, BC + tb, :]).then_inc(v0_ev, 1)

                def kev0(u):
                    jj = u // 4 * 2 + u % 2
                    dve.wait_ge(k0_ps, u0 + (u + 1))
                    for i in (0, 1):
                        rows = slice(32 * i, 32 * i + 32)
                        for e in range(2):
                            ins = V_.tensor_scalar(KZ[rows, :, 2 * i + e, :], PS[rows, BB, :].rearrange("p (b t) -> p b t", t=P),
                                                   VEC[rows, COL_BK0 + jj:COL_BK0 + jj + 1],
                                                   VEC[rows, COL_EVEN + e:COL_EVEN + e + 1], ALU.add, ALU.mult)
                    ins.then_inc(k0_ev, 1)

                def soft0(s):
                    u, b = s // 4, s % 4
                    tile = u // 2 % 2 * BT + b
                    dve.wait_ge(s0_ps, s0 + (s + 1))
                    V_.tensor_tensor(P0[s % 3].rearrange("p (a h t) -> p a h t", a=2, t=P),
                                     PS[:, BS:BS + 2, :].rearrange("p a (h t) -> p a h t", t=P),
                                     BIASVR[:, tile * P:(tile + 1) * P].unsqueeze(1).unsqueeze(1).to_broadcast([P, 2, 4, P]),
                                     ALU.add).then_inc(z0, 1)
                    dve.wait_ge(z0, s0 + (s + 1))
                    V_.tensor_reduce(MX[:, s % 3, :], P0[s % 3].rearrange("p (h t) -> p h t", t=P),
                                     AXX, ALU.max, negate=True).then_inc(max0, 1)

                def rec0(s):
                    dve.wait_ge(exp0, s0 + (s + 1))
                    V_.reciprocal(RC[:, s % 2, :], SUM0[:, s % 2, :]).then_inc(rc0, 1)

                def cxlo0(s):
                    u, b = s // 4, s % 4
                    jj = u // 4 * 2 + u % 2
                    dve.wait_ge(cx0_hi, s0 + (s + 1))
                    V_.scalar_tensor_tensor(CX0[:, u % 2, 1, b * P:(b + 1) * P], PS[:, BB, 0:P],
                                            VEC[:, COL_BV0 + jj:COL_BV0 + jj + 1],
                                            CX0[:, u % 2, 0, b * P:(b + 1) * P].bitcast(F32), ALU.add, ALU.subtract).then_inc(cx0_lo, 1)

                def add_rows(bank, tile, filled, count, done):
                    dve.wait_ge(filled, count)
                    V_.tensor_tensor(X[:, tile, :], PS[:, bank, :], X[:, tile, :], ALU.add).then_inc(done, 1)

                def add0(n):
                    for t in range(BT):
                        add_rows(BC + t % 2, n % 2 * BT + t, o0_ps, o0 + (n * BT + t + 1), xadd0)

                V_.memset(KZ[:], 0.0).then_inc(zeros_done, 1)
                V_.memset(VP[:], 0.0).then_inc(zeros_done, 1)
                src(0)
                vsplit(1, nq)
                for i in range(1, 4):
                    src(i)
                vev0(0)
                kev0(0)
                vev0(1)
                dve.wait_ge(ld_rows, hf * 96 + 32)
                soft0(0)
                soft0(1)
                rec0(0)
                dve.wait_ge(bo_added, hf * 8 + 2)
                for s in range(STEPS0):
                    u, b = s // 4, s % 4
                    if s + 1 < STEPS0:
                        rec0(s + 1)
                    if s + 2 < STEPS0:
                        soft0(s + 2)
                    if b == 1 and u + 1 < UNITS0:
                        kev0(u + 1)
                    if s % 8 == 1 and s > 1:
                        add0(s // 8 - 1)
                    if s:
                        cxlo0(s - 1)
                    if s == 10:
                        vsplit(1, nq + 1)
                cxlo0(STEPS0 - 1)
                add0(3)

                def step(r, k, ins):
                    ins.then_inc(ln_step, 1)
                    dve.wait_ge(ln_step, r * 8 + k)

                def norm_x(r, tb, eps):
                    for b in range(BT):
                        ins = V_.bn_stats(BNS[:, b, :], X[:, tb * BT + b, :])
                    step(r, 1, ins)
                    take_wait(dve)
                    for b in range(BT):
                        ins = V_.bn_aggr(MV[:, b, :], BNS[:, b, :])
                    step(r, 2, ins)
                    V_.tensor_scalar(NT[:], MV[:, :, 1], eps, None, ALU.add).then_inc(ln_step, 1)
                    dve.wait_ge(sd_done, r + 1)
                    step(r, 4, V_.reciprocal(RS[:], SD[:]))
                    step(r, 5, V_.tensor_tensor(SUM[:], RS[:], RS[:], ALU.mult))
                    step(r, 6, V_.tensor_tensor(NT[:], NT[:], SUM[:], ALU.mult))
                    step(r, 7, V_.tensor_scalar(NT[:], NT[:], -0.5, 1.5, ALU.mult, ALU.add))
                    step(r, 8, V_.tensor_tensor(RS[:], RS[:], NT[:], ALU.mult))
                    for b in range(BT):
                        ins = V_.tensor_scalar(XN[:, b, :], X[:, tb * BT + b, :], MV[:, b, 0:1], RS[:, b:b + 1],
                                               ALU.subtract, ALU.mult)
                    return ins

                def norm(hf, i, eps, scale_col, off_col):
                    for tb in range(TB):
                        t = norm_index(hf, i) * TB + tb
                        dve.wait_ge(tr_ps, t * C)
                        norm_x((hf * 4 + (i + 1)) * 2 + tb, tb, eps).then_inc(xn_done, 1)

                        def low(c):
                            dve.wait_ge(at_hi, t * C + (c + 1))
                            V_.tensor_tensor(AT[:, 1, c, tb * BTOK:(tb + 1) * BTOK], HF[:, c % 2, :],
                                             AT[:, 0, c, tb * BTOK:(tb + 1) * BTOK].bitcast(F32), ALU.subtract).then_inc(at_lo, 1)

                        for c in range(C):
                            if c >= 2:
                                low(c - 2)
                                dve.wait_ge(at_lo, t * C + (c - 1))
                            dve.wait_ge(tr_ps, t * C + (c + 1))
                            V_.tensor_scalar(HF[:, c % 2, :], PS[:, c, :], VEC[:, bass.ds(scale_col + c, 1)],
                                             VEC[:, bass.ds(off_col + c, 1)], ALU.mult, ALU.add).then_inc(f_done, 1)
                        low(2)
                        low(3)

                dve.wait_ge(xadd0, o0 + 16)
                for tb in range(TB):
                    if tb:
                        dve.wait_ge(free_done, hf * 2 + 1)
                    ins = norm_x(hf * 8 + tb, tb, 1e-6)
                    ins.then_inc(vb_done, 1)
                    dve.wait_ge(vb_done, hf * 6 + (2 * tb + 1))
                    V_.tensor_tensor(XN[:], XN[:], BVR[:, 0:D].unsqueeze(1).to_broadcast([P, BT, D]), ALU.mult).then_inc(vb_done, 1)
                    dve.wait_ge(vb_done, hf * 6 + (2 * tb + 2))
                    V_.tensor_tensor(X[:, tb * BT:(tb + 1) * BT, :], XN[:], BVR[:, D:2 * D].unsqueeze(1).to_broadcast([P, BT, D]),
                                     ALU.add).then_inc(free_done, 1)
                dve.wait_ge(free_done, hf * 2 + 2)
                take_wait(dve)

                with dve.Fori(0, LAYERS, 1) as ly:
                    b0 = half_units(hf, ly)
                    lq = nq + G0 + ly * G1
                    cols = ly * LAYER_COLS + COL_LAYER
                    dve.wait_ge(xadd, b0 * BT)
                    norm(hf, ly, 1e-5, cols + COL_SCALE, cols + COL_OFF)
                    vsplit(1, lq)
                    dve.wait_ge(ld_rows, (hf * 6 + ly * 2) * 16 + 64)
                    V_.tensor_tensor(BVR[:], BVR[:], BIASVR[:], ALU.subtract).then_inc(vb_done, 1)
                    dve.wait_ge(vb_done, hf * 6 + ly + 5)

                    def kev(n, h, head):
                        V_.tensor_copy(K[:, :, P:T1], VEC[:, bass.ds(cols + head + COL_BIASK, 1)].unsqueeze(1).to_broadcast([P, BT, 1]))
                        dve.wait_ge(k_ps, n * 2 + (h + 1))
                        V_.tensor_scalar(K[:, :, 0:P], PS[:, BB, :].rearrange("p (b t) -> p b t", t=P),
                                         VEC[:, bass.ds(cols + head + COL_BK, 1)], None, ALU.add).then_inc(k_ev, 1)

                    def vev(n, tb, g):
                        for i in range(2):
                            dve.wait_ge(v_ps, n * 2 + (i + 1))
                            V_.tensor_tensor(V[:, tb, 2 * i:2 * i + 2, :], PS[:, BC + i, :].rearrange("p (b d) -> p b d", d=256),
                                             BVR[:, bass.ds(g * 256, 256)].unsqueeze(1).to_broadcast([P, 2, 256]),
                                             ALU.add).then_inc(v_ev, 1)

                    def soft(n, h):
                        dve.wait_ge(s_ps, n * 2 + (h + 1))
                        V_.tensor_reduce(MX[:, 0, 0:BT].rearrange("p (a b) -> p a b", a=2),
                                         PS[:, BS:BS + 2, :].rearrange("p a (b t) -> p a b t", b=2)[:, :, :, 0:T1],
                                         AXX, ALU.max, negate=True).then_inc(max_done, 1)
                        dve.wait_ge(exp_done, n * 2 + (h + 1))
                        V_.reciprocal(RC[:, 0, 0:BT], SUM[:]).then_inc(rc_done, 1)

                    def body(g, first, last):
                        for tb in range(TB):
                            n = b0 + g * TB + tb
                            end = last and tb == 1
                            for h in range(2):
                                soft(n, h)
                                if h == 0:
                                    kev(n, 1, g * 2 + 1)
                                    if tb == 1 and not last:
                                        vsplit(1, lq + g + 1)
                                    if not (first and tb == 0):
                                        for t in range(BT):
                                            add_rows(BC + t % 2, (1 - tb) * BT + t, o_ps, n * BT + (t - BT + 1), xadd)
                                elif not end:
                                    kev(n + 1, 0, g * 2 + 2 * tb)
                                    vev(n + 1, 1 - tb, g + tb)
                                dve.wait_ge(cx_hi, n * 2 + (h + 1))
                                V_.scalar_tensor_tensor(CX[:, h, 1, :], PS[:, BPV, :],
                                                        VEC[:, bass.ds(cols + g * 2 + (COL_BIASV + h), 1)],
                                                        CX[:, h, 0, :].bitcast(F32), ALU.add, ALU.subtract).then_inc(cx_lo, 1)

                    kev(b0, 0, 0)
                    vev(b0, 0, 0)
                    body(0, True, False)
                    with dve.Fori(1, G1 - 1, 1) as g:
                        body(g, False, False)
                    body(G1 - 1, False, True)
                    for t in range(BT):
                        add_rows(BC + t % 2, BT + t, o_ps, (b0 + (NB1 - 1)) * BT + (t + 1), xadd)

                dve.wait_ge(xadd, half_units(hf, LAYERS) * BT)
                norm(hf, LAYERS, 1e-5, COL_MLP_SCALE, COL_MLP_OFF)
                dve.wait_ge(bo_added, hf * 8 + 8)
                take_wait(dve)
                with dve.Fori(0, FG // 2, 1) as gp:
                    m0 = hf * FG * TB + gp * 4

                    def hsplit(m):
                        for f in range(2):
                            dve.wait_ge(gelu_done, m0 * 2 + (2 * m + f + 1))
                            V_.tensor_copy(HB[:, m % 2, f, 0, :], HF[:, f, :]).then_inc(h_hi, 1)
                            dve.wait_ge(h_hi, m0 * 2 + (2 * m + f + 1))
                            V_.tensor_tensor(HB[:, m % 2, f, 1, :], HF[:, f, :], HB[:, m % 2, f, 0, :].bitcast(F32),
                                             ALU.subtract).then_inc(h_lo, 1)

                    def madd_(m):
                        for t in range(BT):
                            add_rows(BC + t % 2, m % 2 * BT + t, m_ps, m0 * BT + (m * BT + t + 1), madd)

                    hsplit(0)
                    for m in range(1, 4):
                        hsplit(m)
                        madd_(m - 1)
                    madd_(3)


def _slabs(np, w, n):
    k, cols = w.shape
    return w.reshape(k // P, P, cols // n, n).transpose(2, 1, 0, 3).reshape(cols // n, P, k // P * n)


def _row_slabs(np, w):
    return w.reshape(-1, 2, P, D).transpose(0, 2, 1, 3).reshape(-1, P, 2 * D)


def _layout(np, a):
    halves = lambda x: x.reshape(HALVES, TB, BT, P, C, P).transpose(0, 1, 5, 4, 2, 3).reshape(HALVES, TB, P, C, BTOK)
    kv_cols = np.arange(NH0 * HD0) // 64 * HD0 + np.arange(NH0 * HD0) % HD0
    pair = lambda n: (a[f"L1_xattn_{n}1"], a[f"L1_xattn_{n}2"])
    w1, w2 = _slabs(np, a["L1_xattn_w_fc1"], 256), _row_slabs(np, a["L1_xattn_w_fc2"])
    per = lambda v: v.reshape(-1, P).T
    odd = (np.arange(P) // HD0 % 2).astype(np.float32)
    cols = [per(a["L0_xattn_bq"]), per(a["L0_xattn_bk"][kv_cols]), per(a["L0_xattn_bv"][kv_cols]),
            (np.float32(1) - odd)[:, None], odd[:, None], per(a["L1_xattn_ln_mlp_scale"]),
            per(a["L1_xattn_ln_mlp_offset"]), per(a["L1_xattn_b_fc1"])]
    for i in (1, 2):
        cols += [per(a[f"L1_xattn_{n}{i}"]) for n in ("bq", "bk", "bias_k", "bias_v")]
        cols += [per(a[f"L1_xattn_ln{i}_{n}"]) for n in ("scale", "offset")]
    return {
        "x": a["x"].reshape(HALVES, SEQ, P, D),
        "xT": halves(a["x"]),
        "cT": halves(a["ctx_2048"]),
        "mask": a["mask_Bx1xSxS2_ff0"].reshape(HALVES, SEQ, P, P).transpose(0, 2, 1, 3),
        "wq": np.concatenate([_slabs(np, a["L0_xattn_Wq"], 256)] + [_slabs(np, w, 256) for w in pair("wq")] + [w1[0::2]]),
        "wk": np.concatenate([_slabs(np, a["L0_xattn_Wk"][:, kv_cols], 256)] + [_slabs(np, w, 256) for w in pair("wk")] + [w1[1::2]]),
        "wv0": _slabs(np, a["L0_xattn_Wv"], P)[0],
        "wv": np.concatenate([_slabs(np, w, 256) for w in pair("wv")] + [w2[0::2]]),
        "wo": np.concatenate([_row_slabs(np, a["L0_xattn_Wo"])] + [_row_slabs(np, w) for w in pair("wo")] + [w2[1::2]]),
        "vec": np.concatenate(cols, axis=1),
        "ident": np.eye(P, dtype=np.float32),
        "gb_rows": np.concatenate([a["L0_xattn_gamma"], a["L0_xattn_beta"]])[None],
        "bo_rows": np.stack([a["L0_xattn_bo"], a["L1_xattn_bo1"], a["L1_xattn_bo2"], a["L1_xattn_b_fc2"]]),
        "bv_rows": np.stack(pair("bv")),
        "biasv_rows": np.stack([v.reshape(-1) for v in pair("bias_v")]),
    }


def kernel(**inputs):
    import numpy as np
    import concourse.bacc as bacc
    from concourse.bass_utils import run_bass_kernel_spmd

    laid = _layout(np, {k: np.asarray(v) for k, v in inputs.items()})
    nc = bacc.Bacc("TRN2", target_bir_lowering=False, num_devices=1)
    arrays, args = {}, []
    for name, a in laid.items():
        a = np.ascontiguousarray(a)
        arrays[f"in_{name}"] = a
        args.append(nc.dram_tensor(f"in_{name}", a.shape, mybir.dt.from_np(a.dtype), kind="ExternalInput").ap())
    args.append(nc.dram_tensor("out_0", (HALVES, SEQ, P, D), F32, kind="ExternalOutput").ap())
    build(nc, *args)
    r = run_bass_kernel_spmd(nc, [arrays], core_ids=[0])
    return r.results[0]["out_0"].reshape(HALVES * SEQ, P, D)
```

```python
from contextlib import ExitStack

import concourse.bass as bass
from concourse import mybir

P = 128
F32 = mybir.dt.float32
F32R = mybir.dt.float32r
ALU = mybir.AluOpType
ACT = mybir.ActivationFunctionType
AXX = mybir.AxisListType.X

PASSES = ((0, 0), (0, 1), (1, 0))

D = 512
C = D // P
HALVES = 2
SEQ = 8
TB = 2
BT = SEQ // TB
BTOK = BT * P

NH0, HD0 = 32, 16
G0 = 2
UNITS0 = 2 * TB * G0
STEPS0 = UNITS0 * BT
ROWS0 = G0 * SEQ
LAYERS = 2
H1, K1 = 16, 128
G1 = H1 // 2
T1 = P + 1
NB1 = G1 * TB
FG = 8

Q_SLABS = G0 + LAYERS * G1 + FG // 2
V_SLABS = 1 + LAYERS * G1 + FG // 2

COL_BQ0, COL_BK0, COL_BV0, COL_EVEN, COL_ODD = 0, 4, 8, 12, 13
COL_FC1 = 14
COL_LAYER = 30
COL_BQ, COL_BK, COL_BIASK, COL_BIASV, COL_SCALE, COL_OFF = 0, 16, 32, 48, 64, 68
LAYER_COLS = 72
LAYERS_END = COL_LAYER + LAYERS * LAYER_COLS
COL_MLP_SCALE, COL_MLP_OFF = LAYERS_END + COL_SCALE, LAYERS_END + COL_OFF
COLS = COL_MLP_OFF + C


def build(nc, x, xT, cT, mask, wq, wk, wv0, wv, wo, vec, ident_in, gb_rows, bo_rows, bv_rows, biasv_rows, out):
    ctx = ExitStack()
    with ctx:
        def sb(name, shape, dt=F32):
            return ctx.enter_context(nc.sbuf_tensor(name, shape, dt))

        def sem(name):
            return ctx.enter_context(nc.semaphore(name))

        X = sb("X", [P, SEQ, D])
        CT = sb("CT", [P, 2, C, SEQ * P], F32R)
        AT = sb("AT", [P, 2, C, SEQ * P], F32R)
        W = sb("W", [P, 4, 2, 1024], F32R)
        RAW = sb("RAW", [P, 4, 1024])
        XN = sb("XN", [P, BT, D])
        HF = sb("HF", [P, 2, BTOK])
        BVR = sb("BVR", [P, 2048])
        BIASVR = sb("BIASVR", [P, 2048])
        BO = sb("BO", [P, D])
        VEC = sb("VEC", [P, COLS])
        BKM = sb("BKM", [P, 2, 4])
        BQS = sb("BQS", [P, 4 + LAYERS * H1])
        IDENT = sb("IDENT", [P, P])
        BNS = sb("BNS", [P, BT, 6])
        MV = sb("MV", [P, BT, 2])
        RS = sb("RS", [P, BT])
        NT = sb("NT", [P, BT])
        NS = sb("NS", [P, BT])
        SD = sb("SD", [P, BT])
        MX = sb("MX", [P, 3, 8])
        RC = sb("RC", [P, 2, 8])
        SUM = sb("SUM", [P, BT])
        SUM0 = sb("SUM0", [P, 2, 8])

        ARENA = 43008
        at = (nc.sbuf_base + 31) // 32 * 32
        sb("arena", [P, ARENA // 4])

        def in_arena(name, shape, dt, offset):
            n = 4
            for s in shape[1:]:
                n *= s
            assert offset % 32 == 0 and offset + n <= ARENA, (name, offset, n)
            return nc.alloc_sbuf_tensor_at(name, shape, dt, offset=at + offset)

        KZ = in_arena("KZ", [P, BT, 8, P], F32, 0)
        VP = in_arena("VP", [P, 2, 8, P], F32, 16384)
        CX0 = in_arena("CX0", [P, 2, 2, BTOK], F32R, 24576)
        Q0 = in_arena("Q0", [P, BTOK], F32, 32768)
        V0 = in_arena("V0", [P, SEQ, 8, HD0], F32, 34816)
        PT0A = in_arena("PT0A", [P, 8 * P], F32, 38912)
        P0 = [XN[:, 0:2, :].rearrange("p a n -> p (a n)"), XN[:, 2:4, :].rearrange("p a n -> p (a n)"),
              HF[:].rearrange("p a n -> p (a n)")]
        PT0 = [PT0A[:], BVR[:, 1024:2048]]
        Q = in_arena("Q", [P, BTOK], F32, 0)
        K = in_arena("K", [P, BT, 132], F32, 2048)
        V = in_arena("V", [P, 2, BT, 256], F32, 4160)
        PR = in_arena("PR", [P, BT, 132], F32, 12352)
        PT = in_arena("PT", [P, BTOK], F32, 14464)
        CX = in_arena("CX", [P, 2, 2, BTOK], F32R, 16512)
        HB = in_arena("HB", [P, 2, 2, 2, BTOK], F32R, 0)

        STAGE = [XN[:], X[:, 0:BT, :], X[:, BT:SEQ, :], XN[:]]

        PS = ctx.enter_context(nc.psum_tensor("PS", [P, 8, 512], F32))
        BA, BB, BC, BD, BS, BPT, BPV = 0, 1, 2, 3, 4, 6, 7
        BANKS_END, BANKS_ROWS, BANKS_MLP = (BB, BPT, BPV, BA), (BC, BD, BC, BD), (BS, BS + 1, BPT, BPV)
        LAST_ROWS = (BC, BD, BS, BS + 1)

        ld_vec, ld_ident, ld_x, ld_masks, ld_bo = sem("ld_vec"), sem("ld_ident"), sem("ld_x"), sem("ld_masks"), sem("ld_bo")
        ld_rows = [sem("ld_rows_low"), sem("ld_rows_high")]
        ld_src = [sem(f"ld_src{i}") for i in range(3)]
        ld = [sem(f"ld_{k}") for k in "qkvo"]
        w_hi = [sem(f"w_{k}_hi") for k in "qkvo"]
        w_ready = [sem(f"w_{k}_ready") for k in "qkvo"]
        src_hi, src_lo = sem("src_hi"), sem("src_lo")
        const_done = sem("const_done")
        zeros_done = sem("zeros_done")
        out_done = sem("out_done")
        v0_ps, v0_ev, q0_ps, q0_ev, k0_ps, k0_ev = (sem(n) for n in ("v0_ps", "v0_ev", "q0_ps", "q0_ev", "k0_ps", "k0_ev"))
        k0_ev2 = sem("k0_ev2")
        s0_ps, z0, max0, exp0, rc0, norm0 = (sem(n) for n in ("s0_ps", "z0", "max0", "exp0", "rc0", "norm0"))
        t0_ps, t0_ev, pv0_ps, vp0 = (sem(n) for n in ("t0_ps", "t0_ev", "pv0_ps", "vp0"))
        cx0_hi, cx0_lo, o0_ps = (sem(n) for n in ("cx0_hi", "cx0_lo", "o0_ps"))
        own_mid, own_done = sem("own_mid"), sem("own_done")
        ln_stats, ln_step, sd_done = sem("ln_stats"), sem("ln_step"), sem("sd_done")
        xn_done, tr_ps, f_done, at_hi, at_lo = (sem(n) for n in ("xn_done", "tr_ps", "f_done", "at_hi", "at_lo"))
        bo_added, vb_done = sem("bo_added"), sem("vb_done")
        q_ps, q_ev, k_ps, k_ev, v_ps, v_ev = (sem(n) for n in ("q_ps", "q_ev", "k_ps", "k_ev", "v_ps", "v_ev"))
        s_ps, max_done, exp_done, rc_done, norm_done = (sem(n) for n in ("s_ps", "max_done", "exp_done", "rc_done", "norm_done"))
        t_ps, t_ev, pv_ps, cx_hi, cx_lo, o_ps, xadd = (sem(n) for n in ("t_ps", "t_ev", "pv_ps", "cx_hi", "cx_lo", "o_ps", "xadd"))
        h_ps, gelu_done, h_hi, h_lo, m_ps, madd = (sem(n) for n in ("h_ps", "gelu_done", "h_hi", "h_lo", "m_ps", "madd"))

        waited = sem("waited")

        block = ctx.enter_context(nc.Block())

        def slab3(t, n):
            return t.rearrange("p (c n) -> p c n", n=n)

        def norm_index(hf, ly):
            return hf * (LAYERS + 1) + ly

        def half_units(hf, ly):
            return (hf * LAYERS + ly) * NB1

        def x_count(hf, n):
            return n * BT + (hf + 1) * ROWS0

        def take_wait(eng):
            eng.sem_inc(waited, 1)

        @block.sync
        def _(sp):
            half = lambda t, hf: t[bass.ds(hf, 1)]

            def load_src(hf, i):
                sp.dma_start(STAGE[i], half((cT, xT)[i % 2], hf)[:, i // 2].rearrange("a p c t -> (a p) c t")).then_inc(ld_src[i % 3], 16)

            def load_first_slab(n):
                if n == 2:
                    sp.dma_start(RAW[:, 2, 0:512], wv0).then_inc(ld[2], 16)
                else:
                    sp.dma_start(RAW[:, n, :], (wq, wk, None, wo)[n][0]).then_inc(ld[n], 16)

            def load_half(hf):
                nq, nv = hf * Q_SLABS, hf * V_SLABS
                sp.dma_start(BIASVR[:, 0:SEQ * P].rearrange("p (b t) -> p b t", b=SEQ),
                             half(mask, hf).rearrange("a p b t -> (a p) b t")).then_inc(ld_masks, 16)
                sp.wait_ge(src_lo, hf * 4 + 1)
                load_src(hf, 3)
                load_first_slab(3)
                sp.dma_start(BIASVR[:, 2 * D:4 * D], gb_rows.to_broadcast([P, 2 * D])).then_inc(ld_masks, 16)
                sp.dma_start(BO[:], bo_rows[0:1, :].to_broadcast([P, D])).then_inc(ld_bo, 16)
                sp.wait_ge(src_lo, hf * 4 + 3)
                sp.dma_start(X[:], half(x, hf).rearrange("a b p n -> p (a b) n")).then_inc(ld_x, 16)
                for n in (0, 1, 3):
                    sp.wait_ge(w_ready[n], nq + 1)
                    sp.dma_start(RAW[:, n, :], (wq, wk, None, wo)[n][1]).then_inc(ld[n], 16)

                def load_slabs(i):
                    for n in range(4):
                        s = i + (0 if n == 2 else G0)
                        sp.wait_ge(w_ready[n], s + (nv + 1 if n == 2 else nq))
                        sp.dma_start(RAW[:, n, :], (wq, wk, wv, wo)[n][bass.ds(s, 1)].rearrange("a p n -> (a p) n")).then_inc(ld[n], 16)

                load_slabs(0)
                with sp.Fori(0, LAYERS, 1) as ly:
                    sp.wait_ge(xn_done, norm_index(hf, ly) * TB + 1)
                    for part in range(2):
                        if part:
                            sp.wait_ge(own_done, hf * TB + TB)
                        for rows, row in ((BVR, bv_rows), (BIASVR, biasv_rows)):
                            sp.dma_start(rows[:, part * 1024:(part + 1) * 1024],
                                         row[bass.ds(ly, 1), part * 1024:(part + 1) * 1024].to_broadcast([P, 1024])).then_inc(ld_rows[part], 16)
                    sp.wait_ge(bo_added, (hf * 4 + ly + 1) * TB)
                    sp.dma_start(BO[:], bo_rows[bass.ds(ly + 1, 1), :].to_broadcast([P, D])).then_inc(ld_bo, 16)
                    with sp.Fori(1, G1 + 1, 1) as g:
                        load_slabs(ly * G1 + g)
                sp.wait_ge(bo_added, (hf * 4 + 3) * TB)
                sp.dma_start(BO[:], bo_rows[3:4, :].to_broadcast([P, D])).then_inc(ld_bo, 16)
                with sp.Fori(1, FG // 2, 1) as gp:
                    load_slabs(gp + LAYERS * G1)

            def store(hf, tb):
                sp.wait_ge(madd, (hf + 1) * FG * TB * BT - (TB - 1 - tb) * 2 * BT)
                sp.dma_start(half(out, hf)[:, tb * BT:(tb + 1) * BT].rearrange("a b p n -> p (a b) n"),
                             X[:, tb * BT:(tb + 1) * BT, :]).then_inc(out_done, 16)

            load_src(0, 0)
            sp.dma_start(VEC[:], vec).then_inc(ld_vec, 16)
            load_first_slab(2)
            load_src(0, 1)
            load_first_slab(0)
            load_first_slab(1)
            sp.dma_start(IDENT[:], ident_in).then_inc(ld_ident, 16)
            load_src(0, 2)
            with sp.Fori(0, HALVES - 1, 1) as hf:
                load_half(hf)
                for n in (2, 0, 1):
                    sp.wait_ge(w_ready[n], (hf + 1) * (V_SLABS if n == 2 else Q_SLABS))
                    load_first_slab(n)
                sp.wait_ge(tr_ps, norm_index(hf + 1, 0) * TB * C)
                load_src(hf + 1, 0)
                for tb in range(TB):
                    store(hf, tb)
                    sp.wait_ge(out_done, hf * TB * 16 + (tb + 1) * 16)
                    load_src(hf + 1, 1 + tb)
            load_half(HALVES - 1)
            for tb in range(TB):
                store(HALVES - 1, tb)
            sp.wait_ge(out_done, HALVES * TB * 16)

        def split(eng, hi_op, n, count, width=1024):
            eng.wait_ge(ld[n], count * 16 + 16)
            take_wait(eng)
            hi_op(W[:, n, 0, 0:width], RAW[:, n, 0:width]).then_inc(w_hi[n], 1)
            eng.wait_ge(w_hi[n], count + 1)
            eng.tensor_tensor(W[:, n, 1, 0:width], RAW[:, n, 0:width],
                              W[:, n, 0, 0:width].bitcast(F32), ALU.subtract).then_inc(w_ready[n], 1)

        @block.gpsimd
        def _(pool):
            def copy_hi(out, in_):
                return nc.gpsimd.tensor_scalar(out, in_, 1.0, 0.0, ALU.mult, ALU.add)

            def psplit(n, count, width=1024):
                split(nc.gpsimd, copy_hi, n, count, width)

            def add_bo(tb):
                nc.gpsimd.tensor_tensor(X[:, tb * BT:(tb + 1) * BT, :], X[:, tb * BT:(tb + 1) * BT, :],
                                        BO[:].unsqueeze(1).to_broadcast([P, BT, D]), ALU.add).then_inc(bo_added, 1)

            with pool.Fori(0, HALVES, 1) as hf:
                nq, nv = hf * Q_SLABS, hf * V_SLABS
                psplit(2, nv, 512)
                psplit(0, nq)
                psplit(3, nq)
                pool.wait_ge(ld_bo, hf * 64 + 16)
                pool.wait_ge(ld_x, hf * 16 + 16)

                def norm(s):
                    pool.wait_ge(rc0, hf * STEPS0 + (s + 1))
                    z = P0[s % 3].rearrange("p (h t) -> p h t", t=P)
                    nc.gpsimd.tensor_tensor(z, z, RC[:, s % 2, :].unsqueeze(2).to_broadcast([P, 8, P]),
                                            ALU.mult).then_inc(norm0, 1)

                def pad(s):
                    u, b = s // 4, s % 4
                    jj = u // 4 * 2 + u % 2
                    if s == 0:
                        pool.wait_ge(v0_ev, hf * 2 + 1)
                        pool.wait_ge(zeros_done, hf * 2 + 2)
                    if s == 8:
                        pool.wait_ge(v0_ev, hf * 2 + 2)
                    if s >= 2:
                        pool.wait_ge(pv0_ps, hf * STEPS0 + (s - 1))
                    v = V0[:, u // 2 % 2 * BT + b, 2 * jj:2 * jj + 2, :]
                    take_wait(pool)
                    for h in range(8):
                        ins = nc.gpsimd.tensor_copy(VP[:, s % 2, h, h * HD0:(h + 1) * HD0], v[:, h // 4, :])
                    ins.then_inc(vp0, 1)

                for tb in range(TB):
                    add_bo(tb)
                norm(0)
                for s in range(STEPS0):
                    if s + 1 < STEPS0:
                        norm(s + 1)
                    pad(s)
                    if s == 10:
                        pool.wait_ge(q0_ps, hf * UNITS0 + 4)
                        psplit(0, nq + 1)
                    if s == 18:
                        pool.wait_ge(o0_ps, hf * ROWS0 + 8)
                        psplit(3, nq + 1)
                pool.wait_ge(q0_ps, (hf + 1) * UNITS0)
                psplit(0, nq + G0)
                psplit(2, nv + 1)
                with pool.Fori(0, LAYERS, 1) as ly:
                    b0 = half_units(hf, ly)
                    lq, lv = nq + G0 + ly * G1, nv + 1 + ly * G1

                    def sub_rows(part):
                        pool.wait_ge(ld_rows[part], (hf * LAYERS + ly) * 32 + 32)
                        nc.gpsimd.tensor_tensor(BVR[:, part * 1024:(part + 1) * 1024], BVR[:, part * 1024:(part + 1) * 1024],
                                                BIASVR[:, part * 1024:(part + 1) * 1024], ALU.subtract).then_inc(vb_done, 1)

                    def add_layer_bo(tb):
                        pool.wait_ge(xn_done, norm_index(hf, ly) * TB + (tb + 1))
                        add_bo(tb)

                    sub_rows(0)
                    pool.wait_ge(ld_bo, (hf * 4 + ly) * 16 + 32)
                    add_layer_bo(0)

                    def weights(n, h):
                        pool.wait_ge(rc_done, n * 2 + (h + 1))
                        nc.gpsimd.tensor_tensor(PR[:, :, 0:P], PR[:, :, 0:P],
                                                RC[:, 0, 0:BT].unsqueeze(2).to_broadcast([P, BT, P]),
                                                ALU.mult).then_inc(norm_done, 1)

                    def body(g, first, last):
                        n = b0 + g * TB
                        weights(n, 0)
                        if first:
                            add_layer_bo(1)
                            sub_rows(1)
                        else:
                            pool.wait_ge(o_ps, n * BT)
                        psplit(3, lq + g)
                        weights(n, 1)
                        n = b0 + g * TB + 1
                        weights(n, 0)
                        if last:
                            weights(n, 1)
                        pool.wait_ge(q_ps, n * 2 + 2)
                        psplit(0, lq + g + 1)
                        psplit(2, lv + g + 1)
                        if not last:
                            weights(n, 1)

                    body(0, True, False)
                    with pool.Fori(1, G1 - 1, 1) as g:
                        body(g, False, False)
                    body(G1 - 1, False, True)
                lq, lv = nq + G0 + LAYERS * G1, nv + 1 + LAYERS * G1
                mlp_norm = norm_index(hf, LAYERS) * TB
                pool.wait_ge(ld_bo, hf * 64 + 64)
                pool.wait_ge(xn_done, mlp_norm + 1)
                add_bo(0)
                pool.wait_ge(o_ps, half_units(hf, LAYERS) * BT)
                psplit(3, lq)
                pool.wait_ge(xn_done, mlp_norm + 2)
                add_bo(1)
                with pool.Fori(1, FG // 2, 1) as gp:
                    before = hf * FG * TB + gp * 4 - 4
                    for n in (0, 1, 2, 3):
                        if n < 2:
                            pool.wait_ge(h_ps, before * 2 + (6, 8)[n])
                        else:
                            pool.wait_ge(m_ps, before * BT + (12, 16)[n - 2])
                        psplit(n, (lv if n == 2 else lq) + gp)
                pool.wait_ge(m_ps, (hf + 1) * FG * TB * BT)

        @block.tensor
        def _(pe):
            def triple(out, lhs, rhs, chunks, fresh=None):
                k, total = 0, chunks * len(PASSES)
                for c in range(chunks):
                    if fresh is not None:
                        pe.wait_ge(at_lo, fresh + (c + 1))
                    for a, b in PASSES:
                        ins = nc.tensor.matmul(out, lhs(c, a), rhs(c, b), start=(k == 0), stop=(k == total - 1))
                        k += 1
                return ins

            def project(bank, kind, width, col, src, tb, done, fresh=None):
                w = W[:, kind].rearrange("p a (c n) -> p a c n", n=width)
                triple(PS[:, bank, :], lambda c, a: w[:, a, c, col:col + P],
                       lambda c, b: src[:, b, c, tb * BTOK:(tb + 1) * BTOK], C, fresh).then_inc(done, 1)

            pe.wait_ge(ld_ident, 16)
            with pe.Fori(0, HALVES, 1) as hf:
                nq, nv = hf * Q_SLABS, hf * V_SLABS
                u0, s0 = hf * UNITS0, hf * STEPS0
                x0 = hf * (ROWS0 + LAYERS * NB1 * BT)

                def v0(tb):
                    pe.wait_ge(src_lo, hf * 4 + (2 * tb + 1))
                    pe.wait_ge(w_ready[2], nv + 1)
                    w = W[:, 2, :, 0:C * P].rearrange("p a (c n) -> p a c n", n=P)
                    for b in range(BT):
                        t = (tb * BT + b) * P
                        ins = triple(PS[:, BC + tb, b * P:(b + 1) * P], lambda c, a: CT[:, a, c, t:t + P],
                                     lambda c, b_: w[:, b_, c, :], C)
                    ins.then_inc(v0_ps, 1)

                def qk0(u):
                    g, tb, j = u // 4, u // 2 % 2, u % 2
                    if u < 4 and j == 0:
                        pe.wait_ge(src_lo, hf * 4 + (2 * tb + 2))
                    pe.wait_ge(w_ready[0], nq + (g + 1))
                    pe.wait_ge(w_ready[1], nq + (g + 1))
                    project(BB, 1, 256, j * P, CT, tb, k0_ps)
                    if u >= 2:
                        pe.wait_ge(cx0_lo, s0 + (4 * u - 4))
                    project(BA, 0, 256, j * P, AT, tb, q0_ps)

                def s0_(s):
                    u, b = s // 4, s % 4
                    pe.wait_ge(q0_ev, u0 + (u + 1))
                    pe.wait_ge(k0_ev, u0 + (u + 1))
                    pe.wait_ge(k0_ev2, u0 + (u + 1))
                    if s:
                        pe.wait_ge(z0, s0 + s)
                    for i in range(2):
                        ins = nc.tensor.matmul(PS[:, BS + i, :], Q0[:, b * P:(b + 1) * P],
                                               KZ[:, b, 4 * i:4 * i + 4, :], start=True, stop=True)
                    ins.then_inc(s0_ps, 1)

                def t0(s):
                    pe.wait_ge(norm0, s0 + (s + 1))
                    if s:
                        pe.wait_ge(t0_ev, s0 + s)
                    for h in range(8):
                        ins = nc.tensor.transpose(PS[:, BPT + h // 4, h % 4 * P:(h % 4 + 1) * P],
                                                  P0[s % 3][:, h * P:(h + 1) * P], IDENT[:])
                    ins.then_inc(t0_ps, 1)

                def pv0(s):
                    pe.wait_ge(t0_ev, s0 + (s + 1))
                    pe.wait_ge(vp0, s0 + (s + 1))
                    if s:
                        pe.wait_ge(cx0_lo, s0 + s)
                    if s % 4 == 0:
                        pe.wait_ge(q0_ev, u0 + min(s // 4 + 2, UNITS0))
                    for h in range(8):
                        ins = nc.tensor.matmul(PS[:, BA, 0:P], VP[:, s % 2, h, :], PT0[s % 2][:, h * P:(h + 1) * P],
                                               start=(h == 0), stop=(h == 7))
                    ins.then_inc(pv0_ps, 1)

                def out0(n):
                    pe.wait_ge(cx0_lo, s0 + (n + 1) * 8)
                    pe.wait_ge(w_ready[3], nq + (n // 2 + 1))
                    w = W[:, 3].rearrange("p a (h n) -> p a h n", n=D)
                    for t in range(BT):
                        if t >= 2:
                            pe.wait_ge(xadd, x0 + (n * BT + t - 1))
                        elif n:
                            pe.wait_ge(xadd, x0 + n * BT)
                        else:
                            pe.wait_ge(v0_ev, hf * 2 + (t + 1))
                        triple(PS[:, BC + t % 2, :], lambda h, a: CX0[:, h, a, t * P:(t + 1) * P],
                               lambda h, b: w[:, b, h, :], 2).then_inc(o0_ps, 1)

                def last_rows(cx, h, done):
                    w = W[:, 3].rearrange("p a (h n) -> p a h n", n=D)
                    for t in range(BT):
                        for i, (a, b) in enumerate(PASSES):
                            ins = nc.tensor.matmul(PS[:, LAST_ROWS[t], :], cx[:, h, a, t * P:(t + 1) * P], w[:, b, h, :],
                                                   start=(h == 0 and i == 0), stop=(h == 1 and i == len(PASSES) - 1))
                        if h:
                            ins.then_inc(done, 1)

                v0(0)
                qk0(0)
                v0(1)
                s0_(0)
                s0_(1)
                for s in range(STEPS0):
                    u, b = s // 4, s % 4
                    if s + 2 < STEPS0:
                        s0_(s + 2)
                    if b == 1 and u + 1 < UNITS0:
                        qk0(u + 1)
                    t0(s)
                    if s % 8 == 1 and s > 1:
                        out0(s // 8 - 1)
                    if s:
                        pv0(s - 1)
                pe.wait_ge(w_ready[3], nq + G0)
                pe.wait_ge(xadd, x0 + ROWS0 - BT)
                last_rows(CX0, 0, o0_ps)
                pv0(STEPS0 - 1)
                pe.wait_ge(cx0_lo, s0 + STEPS0)
                last_rows(CX0, 1, o0_ps)

                def norm_t(i, tb, banks):
                    t = i * TB + tb
                    pe.wait_ge(xn_done, t + 1)
                    for c in range(C):
                        if c >= 2 and banks is BANKS_ROWS:
                            pe.wait_ge(f_done, t * C + (c - 1))
                        for b in range(BT):
                            ins = nc.tensor.transpose(PS[:, banks[c], b * P:(b + 1) * P],
                                                      XN[:, b, c * P:(c + 1) * P], IDENT[:])
                        ins.then_inc(tr_ps, 1)

                norm_t(norm_index(hf, 0), 0, BANKS_END)

                with pe.Fori(0, LAYERS, 1) as ly:
                    b0 = half_units(hf, ly)
                    lq, lv = nq + G0 + ly * G1, nv + 1 + ly * G1
                    at_now = norm_index(hf, ly) * 8

                    def keys(n, tb, h, slab):
                        if h == 0:
                            pe.wait_ge(w_ready[1], slab + 1)
                        project(BB, 1, 256, h * P, CT, tb, k_ps)

                    def queries(n, tb, h, slab, fresh=None):
                        if h == 0:
                            pe.wait_ge(w_ready[0], slab + 1)
                        project(BA, 0, 256, h * P, AT, tb, q_ps, fresh)

                    def qk(n, tb, h, slab, fresh=None):
                        pe.wait_ge(k_ev, n * 2 + h)
                        keys(n, tb, h, slab)
                        pe.wait_ge(q_ev, n * 2 + h)
                        queries(n, tb, h, slab, fresh)

                    def values(n, tb, slab, first):
                        w = W[:, 2].rearrange("p a (c n) -> p a c n", n=256)
                        pe.wait_ge(w_ready[2], slab + 1)
                        for i in range(2):
                            if first == "layer":
                                pe.wait_ge(xadd, x_count(hf, n) + (i - 3))
                            elif not first:
                                pe.wait_ge(xadd, x_count(hf, n) + (i - 5))
                            for b in range(2):
                                t = (tb * BT + 2 * i + b) * P
                                ins = triple(PS[:, BC + i, b * 256:(b + 1) * 256], lambda c, a: CT[:, a, c, t:t + P],
                                             lambda c, b_: w[:, b_, c, :], C)
                            ins.then_inc(v_ps, 1)

                    def scores(n, h, start=False):
                        pe.wait_ge(q_ev, n * 2 + (h + 1))
                        pe.wait_ge(k_ev, n * 2 + (h + 1))
                        if start:
                            pe.wait_ge(xadd, x_count(hf, n))
                        else:
                            pe.wait_ge(exp_done, n * 2 + h)
                        for b in range(BT):
                            ins = nc.tensor.matmul(PS[:, BS + b // 2, b % 2 * 256:b % 2 * 256 + T1],
                                                   Q[:, b * P:(b + 1) * P], K[:, b, 0:T1], start=True, stop=True)
                        ins.then_inc(s_ps, 1)

                    def transposes(n, h, start=False):
                        pe.wait_ge(norm_done, n * 2 + (h + 1))
                        if not start:
                            pe.wait_ge(t_ev, n * 2 + h)
                        for b in range(BT):
                            ins = nc.tensor.transpose(PS[:, BPT, b * P:(b + 1) * P], PR[:, b, 0:P], IDENT[:])
                        ins.then_inc(t_ps, 1)

                    def weigh(n, tb, h, start=False):
                        pe.wait_ge(t_ev, n * 2 + (h + 1))
                        pe.wait_ge(v_ev, n * 2 + 2)
                        if not start:
                            pe.wait_ge(cx_lo, n * 2 + h)
                        for b in range(BT):
                            ins = nc.tensor.matmul(PS[:, BPV, b * P:(b + 1) * P], V[:, tb, b, h * P:(h + 1) * P],
                                                   PT[:, b * P:(b + 1) * P], start=True, stop=True)
                        ins.then_inc(pv_ps, 1)

                    def rows(n, slab, more):
                        w = W[:, 3].rearrange("p a (h n) -> p a h n", n=D)
                        pe.wait_ge(cx_lo, n * 2 + 2)
                        pe.wait_ge(w_ready[3], slab + 1)
                        for t in range(BT):
                            if t < 2:
                                pe.wait_ge(v_ev, n * 2 + (t + 1 + 2 * more))
                            else:
                                pe.wait_ge(xadd, x_count(hf, n) + (t - 1))
                            triple(PS[:, BC + t % 2, :], lambda h, a: CX[:, h, a, t * P:(t + 1) * P],
                                   lambda h, b: w[:, b, h, :], 2).then_inc(o_ps, 1)

                    def body(g, first, last):
                        for tb in range(TB):
                            n = b0 + g * TB + tb
                            end = last and tb == 1
                            start = first and tb == 0
                            scores(n, 0, start)
                            qk(n, tb, 1, lq + g)
                            transposes(n, 0, start)
                            if start:
                                pe.wait_ge(v_ev, n * 2 + 2)
                                norm_t(norm_index(hf, ly), 1, BANKS_ROWS)
                            else:
                                if end:
                                    scores(n, 1)
                                rows(n - 1, lq + g - (1 - tb), 0 if end else 1)
                            weigh(n, tb, 0, start)
                            if not end:
                                scores(n, 1)
                                qk(n + 1, 1 - tb, 0, lq + g + tb, at_now + 4 if start else None)
                            transposes(n, 1)
                            if not end:
                                values(n + 1, 1 - tb, lv + g + tb, start)
                            else:
                                pe.wait_ge(cx_lo, n * 2 + 1)
                                pe.wait_ge(xadd, x_count(hf, n))
                                last_rows(CX, 0, o_ps)
                            weigh(n, tb, 1)

                    pe.wait_ge(f_done, norm_index(hf, ly) * TB * C + 1)
                    keys(b0, 0, 0, lq)
                    values(b0, 0, lv, "layer")
                    pe.wait_ge(f_done, at_now + 4)
                    queries(b0, 0, 0, lq, at_now)
                    body(0, True, False)
                    with pe.Fori(1, G1 - 1, 1) as g:
                        body(g, False, False)
                    body(G1 - 1, False, True)
                    pe.wait_ge(cx_lo, (b0 + NB1) * 2)
                    last_rows(CX, 1, o_ps)
                    norm_t(norm_index(hf, ly) + 1, 0, BANKS_END)

                lq, lv = nq + G0 + LAYERS * G1, nv + 1 + LAYERS * G1
                x_end = x_count(hf, half_units(hf, LAYERS))

                def pair(gp, first):
                    m0 = hf * FG * TB + gp * 4

                    def hidden(m):
                        e, tb = m % 2, m // 2
                        pe.wait_ge(w_ready[e], lq + gp + 1)
                        if first and m == 0:
                            pe.wait_ge(f_done, norm_index(hf, LAYERS) * 8 + 4)
                        for f in range(2):
                            if m:
                                pe.wait_ge(gelu_done, m0 * 2 + (2 * m + f - 1))
                            elif not first:
                                pe.wait_ge(gelu_done, m0 * 2)
                            fresh = norm_index(hf, LAYERS) * 8 + tb * C if first and e == 0 and f == 0 else None
                            project(BA + f, e, 256, f * P, AT, tb, h_ps, fresh)

                    def down(m):
                        e = m % 2
                        w = W[:, 2 + e].rearrange("p a (h n) -> p a h n", n=D)
                        pe.wait_ge(h_lo, m0 * 2 + (2 * m + 2))
                        pe.wait_ge(w_ready[2 + e], (lq if e else lv) + gp + 1)
                        for t in range(BT):
                            if first and m == 0 and t < 2:
                                pe.wait_ge(xadd, x_end + (t - 3))
                            elif m or t:
                                pe.wait_ge(madd, m0 * BT + (m * BT + t - 1))
                            else:
                                pe.wait_ge(madd, m0 * BT)
                            triple(PS[:, BC + t % 2, :], lambda f, a: HB[:, m % 2, f, a, t * P:(t + 1) * P],
                                   lambda f, b: w[:, b, f, :], 2).then_inc(m_ps, 1)

                    hidden(0)
                    for m in range(1, 4):
                        hidden(m)
                        if first and m == 1:
                            pe.wait_ge(xadd, x_end)
                            norm_t(norm_index(hf, LAYERS), 1, BANKS_MLP)
                        down(m - 1)
                    down(3)

                pair(0, True)
                with pe.Fori(1, FG // 2, 1) as gp:
                    pair(gp, False)

        @block.scalar
        def _(act):
            act.wait_ge(ld_vec, 16)
            nc.scalar.activation(BQS[:, 0:4], VEC[:, COL_BQ0:COL_BQ0 + 4], ACT.Copy, scale=HD0 ** -0.5).then_inc(const_done, 1)
            nc.scalar.activation(BQS[:, 4:4 + LAYERS * H1].rearrange("p (l h) -> p l h", l=LAYERS),
                                 VEC[:, COL_LAYER:LAYERS_END].rearrange("p (l n) -> p l n", l=LAYERS)[:, :, COL_BQ:COL_BQ + H1],
                                 ACT.Copy, scale=K1 ** -0.5).then_inc(const_done, 1)
            for e in range(2):
                nc.scalar.activation(BKM[:, e, :], VEC[:, COL_BK0:COL_BK0 + 4], ACT.Copy,
                                     scale=VEC[:, COL_EVEN + e:COL_EVEN + e + 1]).then_inc(const_done, 1)
            act.wait_ge(const_done, 4)
            with act.Fori(0, HALVES, 1) as hf:
                u0, s0 = hf * UNITS0, hf * STEPS0

                def src(i):
                    act.wait_ge(ld_src[i % 3], hf * (32 if i % 3 == 0 else 16) + (32 if i == 3 else 16))
                    tb = i // 2
                    nc.scalar.activation((CT, AT)[i % 2][:, 0, :, tb * BTOK:(tb + 1) * BTOK], STAGE[i], ACT.Copy).then_inc(src_hi, 1)

                def qkev0(u):
                    act.wait_ge(q0_ps, u0 + (u + 1))
                    jj = u // 4 * 2 + u % 2
                    nc.scalar.activation(Q0[:], PS[:, BA, :], ACT.Identity,
                                         bias=BQS[:, jj:jj + 1], scale=HD0 ** -0.5).then_inc(q0_ev, 1)
                    if u == 0:
                        act.wait_ge(zeros_done, hf * 2 + 1)
                    act.wait_ge(k0_ps, u0 + (u + 1))
                    for i in (2, 3):
                        rows = slice(32 * i, 32 * i + 32)
                        for e in range(2):
                            ins = nc.scalar.activation(KZ[rows, :, 2 * i + e, :], PS[rows, BB, :].rearrange("p (b t) -> p b t", t=P),
                                                       ACT.Identity, bias=BKM[rows, e, jj:jj + 1],
                                                       scale=VEC[rows, COL_EVEN + e:COL_EVEN + e + 1])
                    ins.then_inc(k0_ev2, 1)

                def e0(s):
                    act.wait_ge(max0, s0 + (s + 1))
                    if s >= 2:
                        act.wait_ge(rc0, s0 + (s - 1))
                    for h in range(8):
                        ins = nc.scalar.activation(P0[s % 3][:, h * P:(h + 1) * P], P0[s % 3][:, h * P:(h + 1) * P], ACT.Exp,
                                                   bias=MX[:, s % 3, h:h + 1], accum_out=SUM0[:, s % 2, h:h + 1])
                    ins.then_inc(exp0, 1)

                def cxhi0(s):
                    u, b = s // 4, s % 4
                    jj = u // 4 * 2 + u % 2
                    act.wait_ge(pv0_ps, s0 + (s + 1))
                    nc.scalar.activation(CX0[:, u % 2, 0, b * P:(b + 1) * P], PS[:, BA, 0:P], ACT.Identity,
                                         bias=VEC[:, COL_BV0 + jj:COL_BV0 + jj + 1]).then_inc(cx0_hi, 1)

                def root(r):
                    act.wait_ge(ln_step, r * 6 + 2)
                    take_wait(act)
                    nc.scalar.activation(SD[:], NT[:], ACT.Sqrt, scale=-2.0).then_inc(sd_done, 1)

                for i in range(4):
                    src(i)
                qkev0(0)
                e0(0)
                e0(1)
                for s in range(STEPS0):
                    u, b = s // 4, s % 4
                    if b == 1 and u + 1 < UNITS0:
                        qkev0(u + 1)
                    act.wait_ge(t0_ps, s0 + (s + 1))
                    nc.scalar.activation(PT0[s % 2].rearrange("p (a n) -> p a n", a=2), PS[:, BPT:BPT + 2, :],
                                         ACT.Copy).then_inc(t0_ev, 1)
                    if s:
                        cxhi0(s - 1)
                    if s + 2 < STEPS0:
                        e0(s + 2)
                    if s == 26:
                        root(hf * 8)
                    if s == 29:
                        root(hf * 8 + 1)
                cxhi0(STEPS0 - 1)

                def norm_high(i, tb):
                    t = i * TB + tb
                    for c in range(C):
                        act.wait_ge(f_done, t * C + (c + 1))
                        nc.scalar.activation(AT[:, 0, c, tb * BTOK:(tb + 1) * BTOK], HF[:, c % 2, :], ACT.Copy).then_inc(at_hi, 1)

                norm_high(norm_index(hf, 0), 0)
                root(hf * 8 + 2)
                with act.Fori(0, LAYERS, 1) as ly:
                    b0 = half_units(hf, ly)

                    def qev(n, h, head):
                        act.wait_ge(q_ps, n * 2 + (h + 1))
                        take_wait(act)
                        nc.scalar.activation(Q[:], PS[:, BA, :], ACT.Identity,
                                             bias=BQS[:, bass.ds(ly * H1 + head + 4, 1)], scale=K1 ** -0.5).then_inc(q_ev, 1)

                    def exps(n, h):
                        act.wait_ge(max_done, n * 2 + (h + 1))
                        for b in range(BT):
                            ins = nc.scalar.activation(PR[:, b, 0:T1], PS[:, BS + b // 2, b % 2 * 256:b % 2 * 256 + T1],
                                                       ACT.Exp, bias=MX[:, 0, b:b + 1], accum_out=SUM[:, b:b + 1])
                        ins.then_inc(exp_done, 1)

                    def cx_high(n, g, h):
                        act.wait_ge(pv_ps, n * 2 + (h + 1))
                        take_wait(act)
                        nc.scalar.activation(CX[:, h, 0, :], PS[:, BPV, :], ACT.Identity,
                                             bias=VEC[:, bass.ds(ly * LAYER_COLS + g * 2 + (COL_LAYER + COL_BIASV + h), 1)]).then_inc(cx_hi, 1)

                    def body(g, first, last):
                        for tb in range(TB):
                            n = b0 + g * TB + tb
                            end = last and tb == 1
                            for h in range(2):
                                if not (end and h == 1):
                                    exps(n, h)
                                if h == 0:
                                    qev(n, 1, g * 2 + 1)
                                elif not end:
                                    qev(n + 1, 0, g * 2 + 2 * tb)
                                act.wait_ge(t_ps, n * 2 + (h + 1))
                                nc.scalar.activation(PT[:], PS[:, BPT, :], ACT.Copy).then_inc(t_ev, 1)
                                if first and tb == 0 and h == 0:
                                    norm_high(norm_index(hf, ly), 1)
                                if end and h == 0:
                                    exps(n, 1)
                                cx_high(n, g, h)
                                if end and h == 1:
                                    root((hf * 4 + ly + 2) * 2)

                    cols = ly * LAYER_COLS + COL_LAYER
                    act.wait_ge(k_ps, b0 * 2 + 1)
                    take_wait(act)
                    nc.scalar.activation(K[:, :, P:T1], VEC[:, bass.ds(cols + COL_BIASK, 1)].unsqueeze(1).to_broadcast([P, BT, 1]), ACT.Copy)
                    nc.scalar.activation(K[:, :, 0:P], PS[:, BB, :].rearrange("p (b t) -> p b t", t=P), ACT.Identity,
                                         bias=VEC[:, bass.ds(cols + COL_BK, 1)]).then_inc(k_ev, 1)
                    qev(b0, 0, 0)
                    root((hf * 4 + ly + 1) * 2 + 1)
                    body(0, True, False)
                    with act.Fori(1, G1 - 1, 1) as g:
                        body(g, False, False)
                    body(G1 - 1, False, True)
                    norm_high(norm_index(hf, ly) + 1, 0)

                def gelus(gp, first):
                    m0 = hf * FG * TB + gp * 4
                    for m in range(4):
                        for f in range(2):
                            act.wait_ge(h_ps, m0 * 2 + (2 * m + f + 1))
                            if m:
                                act.wait_ge(h_lo, m0 * 2 + (2 * m + f - 1))
                            elif not first:
                                act.wait_ge(h_lo, m0 * 2)
                            take_wait(act)
                            nc.scalar.activation(HF[:, f, :], PS[:, BA + f, :], ACT.Gelu,
                                                 bias=VEC[:, bass.ds(gp * 4 + (COL_FC1 + m % 2 * 2 + f), 1)]).then_inc(gelu_done, 1)
                        if first and m == 1:
                            norm_high(norm_index(hf, LAYERS), 1)

                root((hf + 1) * 8 - 1)
                gelus(0, True)
                with act.Fori(1, FG // 2, 1) as gp:
                    gelus(gp, False)

        @block.vector
        def _(dve):
            V_ = nc.vector
            dve.wait_ge(const_done, 4)

            def vsplit(n, count):
                split(V_, V_.tensor_copy, n, count)

            with dve.Fori(0, HALVES, 1) as hf:
                nq = hf * Q_SLABS
                u0, s0, o0 = hf * UNITS0, hf * STEPS0, hf * ROWS0

                def src(i):
                    dve.wait_ge(src_hi, hf * 4 + (i + 1))
                    tb = i // 2
                    t = (CT, AT)[i % 2]
                    V_.tensor_tensor(t[:, 1, :, tb * BTOK:(tb + 1) * BTOK], STAGE[i],
                                     t[:, 0, :, tb * BTOK:(tb + 1) * BTOK].bitcast(F32), ALU.subtract).then_inc(src_lo, 1)

                def vev0(tb):
                    dve.wait_ge(v0_ps, hf * 2 + (tb + 1))
                    V_.tensor_copy(V0[:, tb * BT:(tb + 1) * BT, :, :].rearrange("p b k d -> p (b k d)"),
                                   PS[:, BC + tb, :]).then_inc(v0_ev, 1)

                def kev0(u):
                    jj = u // 4 * 2 + u % 2
                    if u == 0:
                        dve.wait_ge(zeros_done, hf * 2 + 1)
                    dve.wait_ge(k0_ps, u0 + (u + 1))
                    for i in (0, 1):
                        rows = slice(32 * i, 32 * i + 32)
                        for e in range(2):
                            ins = V_.tensor_scalar(KZ[rows, :, 2 * i + e, :], PS[rows, BB, :].rearrange("p (b t) -> p b t", t=P),
                                                   VEC[rows, COL_BK0 + jj:COL_BK0 + jj + 1],
                                                   VEC[rows, COL_EVEN + e:COL_EVEN + e + 1], ALU.add, ALU.mult)
                    ins.then_inc(k0_ev, 1)

                def soft0(s):
                    u, b = s // 4, s % 4
                    tile = u // 2 % 2 * BT + b
                    dve.wait_ge(s0_ps, s0 + (s + 1))
                    V_.tensor_tensor(P0[s % 3].rearrange("p (a h t) -> p a h t", a=2, t=P),
                                     PS[:, BS:BS + 2, :].rearrange("p a (h t) -> p a h t", t=P),
                                     BIASVR[:, tile * P:(tile + 1) * P].unsqueeze(1).unsqueeze(1).to_broadcast([P, 2, 4, P]),
                                     ALU.add).then_inc(z0, 1)
                    dve.wait_ge(z0, s0 + (s + 1))
                    V_.tensor_reduce(MX[:, s % 3, :], P0[s % 3].rearrange("p (h t) -> p h t", t=P),
                                     AXX, ALU.max, negate=True).then_inc(max0, 1)

                def rec0(s):
                    dve.wait_ge(exp0, s0 + (s + 1))
                    if s >= 2:
                        dve.wait_ge(norm0, s0 + (s - 1))
                    V_.reciprocal(RC[:, s % 2, :], SUM0[:, s % 2, :]).then_inc(rc0, 1)

                def cxlo0(s):
                    u, b = s // 4, s % 4
                    jj = u // 4 * 2 + u % 2
                    dve.wait_ge(cx0_hi, s0 + (s + 1))
                    V_.scalar_tensor_tensor(CX0[:, u % 2, 1, b * P:(b + 1) * P], PS[:, BA, 0:P],
                                            VEC[:, COL_BV0 + jj:COL_BV0 + jj + 1],
                                            CX0[:, u % 2, 0, b * P:(b + 1) * P].bitcast(F32), ALU.add, ALU.subtract).then_inc(cx0_lo, 1)

                def add_rows(bank, tile, filled, count, done):
                    dve.wait_ge(filled, count)
                    V_.tensor_tensor(X[:, tile, :], PS[:, bank, :], X[:, tile, :], ALU.add).then_inc(done, 1)

                def add0(n):
                    for t in range(BT):
                        add_rows(LAST_ROWS[t] if n == 3 else BC + t % 2, n % 2 * BT + t, o0_ps, o0 + (n * BT + t + 1), xadd)

                def stats(tb, tiles, added):
                    for i, b in enumerate(tiles):
                        dve.wait_ge(xadd, added + i)
                        V_.bn_stats(BNS[:, b, :], X[:, tb * BT + b, :]).then_inc(ln_stats, 1)

                def step(r, k, ins):
                    ins.then_inc(ln_step, 1)
                    dve.wait_ge(ln_step, r * 6 + k)

                def variances(r, eps):
                    dve.wait_ge(ln_stats, r * BT + BT)
                    take_wait(dve)
                    for b in range(BT):
                        ins = V_.bn_aggr(MV[:, b, :], BNS[:, b, :])
                    step(r, 1, ins)
                    V_.tensor_scalar(NT[:], MV[:, :, 1], eps, -0.5, ALU.add, ALU.mult).then_inc(ln_step, 1)

                def roots(r):
                    dve.wait_ge(sd_done, r + 1)
                    step(r, 3, V_.reciprocal(RS[:], SD[:]))
                    step(r, 4, V_.tensor_tensor(NT[:], NT[:], RS[:], ALU.mult))
                    step(r, 5, V_.tensor_tensor(NS[:], NT[:], RS[:], ALU.mult))
                    step(r, 6, V_.scalar_tensor_tensor(RS[:], NS[:], 1.5, RS[:], ALU.add, ALU.mult))

                def scales(r, eps):
                    variances(r, eps)
                    roots(r)

                def own(tb, part):
                    if part:
                        dve.wait_ge(own_mid, hf * TB + (tb + 1))
                    for b in range(BT):
                        t = X[:, tb * BT + b, :]
                        if part:
                            ins = V_.scalar_tensor_tensor(t, t, RS[:, b:b + 1], BIASVR[:, 3 * D:4 * D], ALU.mult, ALU.add)
                        else:
                            ins = V_.scalar_tensor_tensor(t, t, MV[:, b, 0:1], BIASVR[:, 2 * D:3 * D], ALU.subtract, ALU.mult)
                    ins.then_inc((own_mid, own_done)[part], 1)

                def own_stats(tb):
                    dve.wait_ge(own_done, hf * TB + (tb + 1))
                    for b in range(BT):
                        V_.bn_stats(BNS[:, b, :], X[:, tb * BT + b, :]).then_inc(ln_stats, 1)

                def apply(tb):
                    for b in range(BT):
                        ins = V_.tensor_scalar(XN[:, b, :], X[:, tb * BT + b, :], MV[:, b, 0:1], RS[:, b:b + 1],
                                               ALU.subtract, ALU.mult)
                    ins.then_inc(xn_done, 1)

                def to_at(i, tb, banks, scale_col, off_col):
                    t = i * TB + tb

                    def low(c):
                        dve.wait_ge(at_hi, t * C + (c + 1))
                        V_.tensor_tensor(AT[:, 1, c, tb * BTOK:(tb + 1) * BTOK], HF[:, c % 2, :],
                                         AT[:, 0, c, tb * BTOK:(tb + 1) * BTOK].bitcast(F32), ALU.subtract).then_inc(at_lo, 1)

                    for c in range(C):
                        if c >= 2:
                            low(c - 2)
                            dve.wait_ge(at_lo, t * C + (c - 1))
                        dve.wait_ge(tr_ps, t * C + (c + 1))
                        V_.tensor_scalar(HF[:, c % 2, :], PS[:, banks[c], :], VEC[:, bass.ds(scale_col + c, 1)],
                                         VEC[:, bass.ds(off_col + c, 1)], ALU.mult, ALU.add).then_inc(f_done, 1)
                    low(2)
                    low(3)

                src(0)
                vsplit(1, nq)
                src(1)
                V_.memset(KZ[:], 0.0).then_inc(zeros_done, 1)
                V_.memset(VP[:], 0.0).then_inc(zeros_done, 1)
                src(2)
                src(3)
                vev0(0)
                kev0(0)
                vev0(1)
                dve.wait_ge(ld_masks, hf * 32 + 32)
                dve.wait_ge(src_lo, hf * 4 + 4)
                soft0(0)
                soft0(1)
                rec0(0)
                dve.wait_ge(bo_added, hf * 8 + 2)
                x0 = hf * (ROWS0 + LAYERS * NB1 * BT)
                for s in range(STEPS0):
                    u, b = s // 4, s % 4
                    if s + 2 < STEPS0:
                        soft0(s + 2)
                    if s + 1 < STEPS0:
                        rec0(s + 1)
                    if b == 1 and u + 1 < UNITS0:
                        kev0(u + 1)
                    if s % 8 == 1 and s > 1:
                        add0(s // 8 - 1)
                    if s:
                        cxlo0(s - 1)
                    if s == 10:
                        vsplit(1, nq + 1)
                    if s == 26:
                        stats(0, range(BT), x0 + 9)
                        variances(hf * 8, 1e-6)
                    if s == 27:
                        roots(hf * 8)
                        own(0, 0)
                    if s == 28:
                        own(0, 1)
                    if s == 29:
                        own_stats(0)
                        variances(hf * 8 + 1, 1e-5)
                    if s == 30:
                        roots(hf * 8 + 1)
                        dve.wait_ge(k0_ps, u0 + UNITS0)
                        vsplit(1, nq + G0)
                dve.wait_ge(t0_ps, s0 + STEPS0)
                apply(0)
                cxlo0(STEPS0 - 1)
                add0(3)
                to_at(norm_index(hf, 0), 0, BANKS_END, COL_LAYER + COL_SCALE, COL_LAYER + COL_OFF)
                stats(1, range(BT), x0 + ROWS0 - BT + 1)
                scales(hf * 8 + 2, 1e-6)
                own(1, 0)
                own(1, 1)
                own_stats(1)

                with dve.Fori(0, LAYERS, 1) as ly:
                    b0 = half_units(hf, ly)
                    lq = nq + G0 + ly * G1
                    cols = ly * LAYER_COLS + COL_LAYER
                    rounds = (hf * 4 + ly + 1) * 2

                    def kev(n, h, head):
                        V_.tensor_copy(K[:, :, P:T1], VEC[:, bass.ds(cols + head + COL_BIASK, 1)].unsqueeze(1).to_broadcast([P, BT, 1]))
                        dve.wait_ge(k_ps, n * 2 + (h + 1))
                        V_.tensor_scalar(K[:, :, 0:P], PS[:, BB, :].rearrange("p (b t) -> p b t", t=P),
                                         VEC[:, bass.ds(cols + head + COL_BK, 1)], None, ALU.add).then_inc(k_ev, 1)

                    def vev(n, tb, g, start=False):
                        for i in range(2):
                            dve.wait_ge(v_ps, n * 2 + (i + 1))
                            if start:
                                dve.wait_ge(vb_done, (hf * LAYERS + ly) * 2 + 1)
                            V_.tensor_tensor(V[:, tb, 2 * i:2 * i + 2, :], PS[:, BC + i, :].rearrange("p (b d) -> p b d", d=256),
                                             BVR[:, bass.ds(g * 256, 256)].unsqueeze(1).to_broadcast([P, 2, 256]),
                                             ALU.add).then_inc(v_ev, 1)

                    def soft(n, h):
                        dve.wait_ge(s_ps, n * 2 + (h + 1))
                        V_.tensor_reduce(MX[:, 0, 0:BT].rearrange("p (a b) -> p a b", a=2),
                                         PS[:, BS:BS + 2, :].rearrange("p a (b t) -> p a b t", b=2)[:, :, :, 0:T1],
                                         AXX, ALU.max, negate=True).then_inc(max_done, 1)
                        dve.wait_ge(exp_done, n * 2 + (h + 1))
                        V_.reciprocal(RC[:, 0, 0:BT], SUM[:]).then_inc(rc_done, 1)

                    def add_block(n, tb, tiles, banks=(BC, BD, BC, BD)):
                        for t in tiles:
                            add_rows(banks[t], tb * BT + t, o_ps, n * BT + (t + 1), xadd)

                    def cx_low(n, g, h):
                        dve.wait_ge(cx_hi, n * 2 + (h + 1))
                        V_.scalar_tensor_tensor(CX[:, h, 1, :], PS[:, BPV, :],
                                                VEC[:, bass.ds(cols + g * 2 + (COL_BIASV + h), 1)],
                                                CX[:, h, 0, :].bitcast(F32), ALU.add, ALU.subtract).then_inc(cx_lo, 1)

                    def body(g, first, last):
                        for tb in range(TB):
                            n = b0 + g * TB + tb
                            end = last and tb == 1
                            start = first and tb == 0
                            soft(n, 0)
                            kev(n, 1, g * 2 + 1)
                            if tb == 1:
                                vsplit(1, lq + g + 1)
                            if start:
                                to_at(norm_index(hf, ly), 1, BANKS_ROWS, cols + COL_SCALE, cols + COL_OFF)
                            else:
                                if end:
                                    soft(n, 1)
                                add_block(n - 1, 1 - tb, range(BT))
                            cx_low(n, g, 0)
                            if end:
                                stats(0, range(BT), x_count(hf, n - 1) + 1)
                                cx_low(n, g, 1)
                                scales(rounds + 2, 1e-5)
                                dve.wait_ge(tr_ps, (norm_index(hf, ly) + 1) * TB * C)
                                apply(0)
                            else:
                                soft(n, 1)
                                kev(n + 1, 0, g * 2 + 2 * tb)
                                vev(n + 1, 1 - tb, g + tb)
                                cx_low(n, g, 1)

                    scales(rounds + 1, 1e-5)
                    dve.wait_ge(tr_ps, (norm_index(hf, ly) * TB + 1) * C)
                    apply(1)
                    vev(b0, 0, 0, True)
                    body(0, True, False)
                    with dve.Fori(1, G1 - 1, 1) as g:
                        body(g, False, False)
                    body(G1 - 1, False, True)
                    n = b0 + (NB1 - 1)
                    add_block(n, 1, range(BT), LAST_ROWS)
                    to_at(norm_index(hf, ly) + 1, 0, BANKS_END, cols + LAYER_COLS + COL_SCALE, cols + LAYER_COLS + COL_OFF)
                    stats(1, range(BT), x_count(hf, n) + 1)

                def pair(gp, first):
                    m0 = hf * FG * TB + gp * 4

                    def hsplit(m):
                        for f in range(2):
                            dve.wait_ge(gelu_done, m0 * 2 + (2 * m + f + 1))
                            V_.tensor_copy(HB[:, m % 2, f, 0, :], HF[:, f, :]).then_inc(h_hi, 1)
                            dve.wait_ge(h_hi, m0 * 2 + (2 * m + f + 1))
                            V_.tensor_tensor(HB[:, m % 2, f, 1, :], HF[:, f, :], HB[:, m % 2, f, 0, :].bitcast(F32),
                                             ALU.subtract).then_inc(h_lo, 1)

                    def madd_(m):
                        if first and m % 2 == 0:
                            dve.wait_ge(bo_added, hf * 8 + (7 + m // 2))
                        for t in range(BT):
                            add_rows(BC + t % 2, m // 2 * BT + t, m_ps, m0 * BT + (m * BT + t + 1), madd)

                    hsplit(0)
                    for m in range(1, 4):
                        hsplit(m)
                        if first and m == 1:
                            dve.wait_ge(h_lo, m0 * 2 + 4)
                            to_at(norm_index(hf, LAYERS), 1, BANKS_MLP, COL_MLP_SCALE, COL_MLP_OFF)
                        madd_(m - 1)
                    madd_(3)

                scales((hf + 1) * 8 - 1, 1e-5)
                dve.wait_ge(tr_ps, (norm_index(hf, LAYERS) * TB + 1) * C)
                apply(1)
                pair(0, True)
                with dve.Fori(1, FG // 2, 1) as gp:
                    pair(gp, False)


def _slabs(np, w, n):
    k, cols = w.shape
    return w.reshape(k // P, P, cols // n, n).transpose(2, 1, 0, 3).reshape(cols // n, P, k // P * n)


def _row_slabs(np, w):
    return w.reshape(-1, 2, P, D).transpose(0, 2, 1, 3).reshape(-1, P, 2 * D)


def _layout(np, a):
    halves = lambda x: x.reshape(HALVES, TB, BT, P, C, P).transpose(0, 1, 5, 4, 2, 3).reshape(HALVES, TB, P, C, BTOK)
    kv_cols = np.arange(NH0 * HD0) // 64 * HD0 + np.arange(NH0 * HD0) % HD0
    pair = lambda n: (a[f"L1_xattn_{n}1"], a[f"L1_xattn_{n}2"])
    w1, w2 = _slabs(np, a["L1_xattn_w_fc1"], 256), _row_slabs(np, a["L1_xattn_w_fc2"])
    per = lambda v: v.reshape(-1, P).T
    odd = (np.arange(P) // HD0 % 2).astype(np.float32)
    cols = [per(a["L0_xattn_bq"]), per(a["L0_xattn_bk"][kv_cols]), per(a["L0_xattn_bv"][kv_cols]),
            (np.float32(1) - odd)[:, None], odd[:, None], per(a["L1_xattn_b_fc1"])]
    for i in (1, 2):
        cols += [per(a[f"L1_xattn_{n}{i}"]) for n in ("bq", "bk", "bias_k", "bias_v")]
        cols += [per(a[f"L1_xattn_ln{i}_{n}"]) for n in ("scale", "offset")]
    cols += [np.zeros((P, COL_SCALE), np.float32), per(a["L1_xattn_ln_mlp_scale"]), per(a["L1_xattn_ln_mlp_offset"])]
    return {
        "x": a["x"].reshape(HALVES, SEQ, P, D),
        "xT": halves(a["x"]),
        "cT": halves(a["ctx_2048"]),
        "mask": a["mask_Bx1xSxS2_ff0"].reshape(HALVES, SEQ, P, P).transpose(0, 2, 1, 3),
        "wq": np.concatenate([_slabs(np, a["L0_xattn_Wq"], 256)] + [_slabs(np, w, 256) for w in pair("wq")] + [w1[0::2]]),
        "wk": np.concatenate([_slabs(np, a["L0_xattn_Wk"][:, kv_cols], 256)] + [_slabs(np, w, 256) for w in pair("wk")] + [w1[1::2]]),
        "wv0": _slabs(np, a["L0_xattn_Wv"], P)[0],
        "wv": np.concatenate([_slabs(np, w, 256) for w in pair("wv")] + [w2[0::2]]),
        "wo": np.concatenate([_row_slabs(np, a["L0_xattn_Wo"])] + [_row_slabs(np, w) for w in pair("wo")] + [w2[1::2]]),
        "vec": np.concatenate(cols, axis=1),
        "ident": np.eye(P, dtype=np.float32),
        "gb_rows": np.concatenate([a["L0_xattn_gamma"], a["L0_xattn_beta"]])[None],
        "bo_rows": np.stack([a["L0_xattn_bo"], a["L1_xattn_bo1"], a["L1_xattn_bo2"], a["L1_xattn_b_fc2"]]),
        "bv_rows": np.stack(pair("bv")),
        "biasv_rows": np.stack([v.reshape(-1) for v in pair("bias_v")]),
    }


def kernel(**inputs):
    import numpy as np
    import concourse.bacc as bacc
    from concourse.bass_utils import run_bass_kernel_spmd

    laid = _layout(np, {k: np.asarray(v) for k, v in inputs.items()})
    nc = bacc.Bacc("TRN2", target_bir_lowering=False, num_devices=1)
    arrays, args = {}, []
    for name, a in laid.items():
        a = np.ascontiguousarray(a)
        arrays[f"in_{name}"] = a
        args.append(nc.dram_tensor(f"in_{name}", a.shape, mybir.dt.from_np(a.dtype), kind="ExternalInput").ap())
    args.append(nc.dram_tensor("out_0", (HALVES, SEQ, P, D), F32, kind="ExternalOutput").ap())
    build(nc, *args)
    r = run_bass_kernel_spmd(nc, [arrays], core_ids=[0])
    return r.results[0]["out_0"].reshape(HALVES * SEQ, P, D)
```
